# Optimizing a Trainium2 kernel written in Bass

```python
import numpy as np
import jax
import jax.numpy as jnp

def _softmax(x, axis=-1):
    return jax.nn.softmax(x, axis=axis)

def _gelu(x):
    return jax.nn.gelu(x, approximate=True)

def _silu(x):
    return jax.nn.silu(x)

def _sigmoid(x):
    return jax.nn.sigmoid(x)

def _layernorm(x, axis=-1, eps=1e-05):
    m = jnp.mean(x, axis=axis, keepdims=True)
    v = jnp.var(x, axis=axis, keepdims=True)
    return (x - m) / jnp.sqrt(v + eps)

def _scatter_add(tgt, idx, src, axis=0):
    return tgt.at[idx].add(src)

def _segment_sum(src, seg, n):
    return jax.ops.segment_sum(src, seg, n)
kernel_name = 'mk_xattn_ffn_d1_seqx_r4_78af33'

def setup_inputs(seed: int=0):
    np.random.seed(seed)
    _w = jnp.asarray

    def _rec_inputs():
        import jax
        import jax.numpy as jnp
        _rk = jax.random.key(seed)
        x = 0.5 + 0.2887 * jax.random.normal(jax.random.fold_in(_rk, 1), (4, 512, 512), jnp.float32)
        _lenS = 512 - jax.random.randint(jax.random.fold_in(_rk, 7), (4,), 0, max(1, 512 // 4) + 1, jnp.int32)
        _lenS2 = 512 - jax.random.randint(jax.random.fold_in(_rk, 8), (4,), 0, max(1, 512 // 4) + 1, jnp.int32)
        _ctx_512P = jax.random.normal(jax.random.fold_in(_rk, 11), (4, 16, 128), jnp.float32)
        _ctx_512c = jax.random.dirichlet(jax.random.fold_in(_rk, 511), 0.3 * jnp.ones((16,), jnp.float32), (4, 512))
        _ctx_512t = jnp.einsum('bsk,bkd->bsd', _ctx_512c, _ctx_512P)
        _ctx_512t = _ctx_512t * jax.lax.rsqrt(jnp.mean(jnp.square(_ctx_512t)) + 1e-12) * 0.953939
        ctx_512 = -0.000392918 + 0.999932 * (_ctx_512t + 0.3 * jax.random.normal(jax.random.fold_in(_rk, 611), (4, 512, 128), jnp.float32))
        return (x, ctx_512)
    x, ctx_512 = _rec_inputs()

    def _L0_xattn_setup():
        import jax, jax.numpy as jnp
        import numpy as np
        B, N, D = (16, 512, 128)
        H = 4
        TOP_K_RATIO = 0.3
        key = jax.random.key(seed)
        k1, k2, k3, k4 = jax.random.split(key, 4)
        h = jax.random.normal(k1, (B, N, D), dtype=jnp.float32)
        adj_raw = jax.random.uniform(k2, (B, N, N), dtype=jnp.float32)
        lim = 1.0 / np.sqrt(D)
        Wq = jax.random.uniform(k3, (D, D), minval=-lim, maxval=lim, dtype=jnp.float32)
        Wk = jax.random.uniform(k4, (D, D), minval=-lim, maxval=lim, dtype=jnp.float32)
        gamma_raw = jnp.float32(-0.85)
        return {'h': h, 'adj_raw': adj_raw, 'Wq': Wq, 'Wk': Wk, 'gamma_raw': gamma_raw}
    _L0_xattn_all = _L0_xattn_setup()
    _L0_xattn_in = {k: v for k, v in _L0_xattn_all.items() if k in ('Wq', 'Wk', 'gamma_raw')}
    del _L0_xattn_all

    def _L0_ffn_setup():
        import jax, jax.numpy as jnp
        import numpy as np
        E = 16
        K = 2
        D = 512
        I = 352
        CAP = 256
        VOCAB = 32320
        key = jax.random.key(seed)
        ks = jax.random.split(key, 11)
        B, S = (4, 256)
        sd = 1.0 / np.sqrt(D)
        si = 1.0 / np.sqrt(I)
        return {'x': jax.random.normal(ks[0], (B, S, D), jnp.float32), 'input_ids': jax.random.randint(ks[1], (B, S), 0, VOCAB, dtype=jnp.int64), 'gate_w': jax.random.normal(ks[2], (E, D), jnp.float32) * sd, 'gate_b': jax.random.normal(ks[3], (E,), jnp.float32) * 0.01, 'W1': jax.random.normal(ks[4], (E, I, D), jnp.float32) * sd, 'W3': jax.random.normal(ks[5], (E, I, D), jnp.float32) * sd, 'W2': jax.random.normal(ks[6], (E, D, I), jnp.float32) * si, 'Ws1': jax.random.normal(ks[7], (I, D), jnp.float32) * sd, 'Ws3': jax.random.normal(ks[8], (I, D), jnp.float32) * sd, 'Ws2': jax.random.normal(ks[9], (D, I), jnp.float32) * si}
    _L0_ffn_all = _L0_ffn_setup()
    _L0_ffn_in = {k: v for k, v in _L0_ffn_all.items() if k in ('input_ids', 'gate_w', 'gate_b', 'W1', 'W3', 'W2', 'Ws1', 'Ws3', 'Ws2')}
    del _L0_ffn_all
    return {'x': x, 'ctx_512': ctx_512, 'L0_xattn_Wq': _L0_xattn_in['Wq'], 'L0_xattn_Wk': _L0_xattn_in['Wk'], 'L0_xattn_gamma_raw': _L0_xattn_in['gamma_raw'], 'L0_ffn_input_ids': _L0_ffn_in['input_ids'], 'L0_ffn_gate_w': _L0_ffn_in['gate_w'], 'L0_ffn_gate_b': _L0_ffn_in['gate_b'], 'L0_ffn_W1': _L0_ffn_in['W1'], 'L0_ffn_W3': _L0_ffn_in['W3'], 'L0_ffn_W2': _L0_ffn_in['W2'], 'L0_ffn_Ws1': _L0_ffn_in['Ws1'], 'L0_ffn_Ws3': _L0_ffn_in['Ws3'], 'L0_ffn_Ws2': _L0_ffn_in['Ws2']}

def reference(x, ctx_512, L0_xattn_Wq, L0_xattn_Wk, L0_xattn_gamma_raw, L0_ffn_input_ids, L0_ffn_gate_w, L0_ffn_gate_b, L0_ffn_W1, L0_ffn_W3, L0_ffn_W2, L0_ffn_Ws1, L0_ffn_Ws3, L0_ffn_Ws2):
    import jax
    import jax.numpy as jnp

    def _L0_xattn_ref(h, adj_raw, Wq, Wk, gamma_raw):
        import jax, jax.numpy as jnp
        import numpy as np
        B, N, D = (16, 512, 128)
        H = 4
        TOP_K_RATIO = 0.3
        b, n, dm = h.shape
        d = dm // H
        Q = (h @ Wq.T).reshape(b, n, H, d).transpose(0, 2, 1, 3)
        K = (h @ Wk.T).reshape(b, n, H, d).transpose(0, 2, 1, 3)
        sim = jnp.einsum('bhnd,bhmd->bnm', Q, K) / (jnp.sqrt(jnp.float32(d)) * H)
        k = max(1, int(n * TOP_K_RATIO))
        topk_vals = jax.lax.top_k(sim, k)[0]
        threshold = topk_vals[:, :, -1:]
        sparse_mask = (sim >= threshold).astype(sim.dtype)
        A_learned = jax.nn.sigmoid(sim) * sparse_mask
        A_learned = (A_learned + jnp.swapaxes(A_learned, -1, -2)) * 0.5
        gamma = jax.nn.sigmoid(gamma_raw)
        return (1.0 - gamma) * adj_raw + gamma * A_learned

    def _L0_ffn_ref(x, input_ids, gate_w, gate_b, W1, W3, W2, Ws1, Ws3, Ws2):
        import jax, jax.numpy as jnp
        import numpy as np
        E = 16
        K = 2
        D = 512
        I = 352
        CAP = 256
        VOCAB = 32320
        shape = x.shape
        xt = x.reshape(-1, D)
        T = xt.shape[0]
        logits = xt.astype(jnp.float32) @ gate_w.astype(jnp.float32).T
        scores = jnp.sqrt(jax.nn.softplus(logits))
        _, idx = jax.lax.top_k(scores + gate_b, K)
        w = jnp.take_along_axis(scores, idx, axis=1)
        w = w / jnp.sum(w, axis=1, keepdims=True)
        e = idx.reshape(-1)
        onehot = jax.nn.one_hot(e, E, dtype=jnp.int32)
        pos = jnp.sum(onehot * (jnp.cumsum(onehot, axis=0) - 1), axis=1)
        valid = pos < CAP
        posc = jnp.where(valid, pos, 0)
        x_pairs = jnp.repeat(xt, K, axis=0)
        x_pairs = jnp.where(valid[:, None], x_pairs, 0.0)
        buf = jnp.zeros((E, CAP, D), xt.dtype).at[e, posc].add(x_pairs)
        g = jnp.einsum('ecd,eid->eci', buf, W1).astype(jnp.float32)
        u = jnp.einsum('ecd,eid->eci', buf, W3).astype(jnp.float32)
        h = (jax.nn.silu(g) * u).astype(xt.dtype)
        out = jnp.einsum('eci,edi->ecd', h, W2)
        y_pairs = out[e, posc] * (w.reshape(-1) * valid)[:, None]
        y = y_pairs.reshape(T, K, D).sum(axis=1)
        gs = jax.nn.silu((xt @ Ws1.T).astype(jnp.float32))
        us = (xt @ Ws3.T).astype(jnp.float32)
        shared = (gs * us).astype(xt.dtype) @ Ws2.T
        return (y + shared).astype(x.dtype).reshape(shape)
    x = x + _L0_xattn_ref(ctx_512, _layernorm(x, axis=-1), L0_xattn_Wq, L0_xattn_Wk, L0_xattn_gamma_raw)
    x = x + _L0_ffn_ref(_layernorm(x, axis=-1), L0_ffn_input_ids, L0_ffn_gate_w, L0_ffn_gate_b, L0_ffn_W1, L0_ffn_W3, L0_ffn_W2, L0_ffn_Ws1, L0_ffn_Ws3, L0_ffn_Ws2)
    return x

_drawn_inputs = setup_inputs


def setup_inputs(seed=0):
    import zlib

    import numpy as np

    out = dict(_drawn_inputs(seed))
    spreads = {}
    factors = {}
    for name, (base, spread) in spreads.items():
        noise = np.random.default_rng([zlib.crc32(name.encode()), seed]).standard_normal(out[name].shape)
        drawn = base * np.exp(spread * noise) if base else spread * noise
        out[name] = jnp.asarray(drawn.astype(out[name].dtype))
    for name, factor in factors.items():
        out[name] = (out[name] * factor).astype(out[name].dtype)
    return out
```

```python
from contextlib import ExitStack

import numpy as np
import concourse.bass as bass
from concourse import mybir

ALU = mybir.AluOpType
ACT = mybir.ActivationFunctionType
AX_X = mybir.AxisListType.X
F32 = mybir.dt.float32
BF16 = mybir.dt.bfloat16
I32 = mybir.dt.int32
U32 = mybir.dt.uint32

P = 128
EPS = 1e-5
HEADS = 4
TOP_K_RATIO = 0.3
CAP = 256
SEARCH_STEPS = 5
BIG = 1e30


class Count:

    def __init__(self):
        self.value = 0

    def up(self, n=1):
        self.value += n
        return self.value


def bank_turns(batches):
    order = []

    def attn(b):
        order.extend([("t0", ("q", b)), ("t1", ("k", b))])
        order.extend((f"t{j % 2}", ("sim", b, j)) for j in range(4))

    attn(0)
    for b in range(batches):
        order.extend((f"t{j % 2}", ("adjT", b, j)) for j in range(4))
        if b + 1 < batches:
            attn(b + 1)
        order.extend((f"t{j % 2}", ("xT", b, j)) for j in range(4))
        order.extend([("s", ("gate", b)), ("s", ("place", b)), ("s", ("table", b))])
    seen, turns = {}, {}
    for bank, name in order:
        turns[name] = (bank, seen.get(bank, 0))
        seen[bank] = seen.get(bank, 0) + 1
    return turns, seen


def build(nc, x, ctxT, WqT, WkT, gamma_raw, gateT, gate_b, W1T, W3T, W2T, Ws1T, Ws3T, Ws2T, out):
    B, N, D = x.shape
    DC = ctxT.shape[1]
    E, _, DK, I = W1T.shape
    T = B * N
    NT = N // P
    TILES = T // P
    MI = -(-I // P)
    LAST = I - (MI - 1) * P
    IP = MI * P
    HALVES = CAP // P
    COLS = E * HALVES
    KTH = max(1, int(N * TOP_K_RATIO))
    SHARED = T // CAP
    SIM_SCALE = 1.0 / (float(np.sqrt(np.float32(DC // HEADS))) * HEADS)
    Z_START, Z_LOW, Z_HIGH = 0.52, -0.3, 1.3
    COUNT_LOW, COUNT_HIGH, COUNT_AIM = 0.618 * N, 0.097 * N, KTH - 4.0
    SAMPLE = N // 2
    assert DC == P and DK == D // P and T % CAP == 0 and HALVES == 2 and NT == 4 and D == N == 512

    x_rows = x.rearrange("b n d -> (b n) d")
    out_rows = out.rearrange("b n d -> (b n) d")
    xn_rows = nc.dram_tensor("xn_rows", [T, D], F32).ap()
    turns, fills = bank_turns(B)

    with ExitStack() as ctx:
        def sb(name, shape, dt=F32):
            return ctx.enter_context(nc.sbuf_tensor(name, shape, dt))

        def sem(name):
            return ctx.enter_context(nc.semaphore(name))

        bank = {n: ctx.enter_context(nc.psum_tensor(f"bank_{n}", [P, 512], F32)) for n in ("t0", "t1", "s")}
        gu_bank = [ctx.enter_context(nc.psum_tensor(f"gu_bank{m}", [P, 512], F32)) for m in range(MI)]
        y_bank = [ctx.enter_context(nc.psum_tensor(f"y_bank{a}", [P, D], F32)) for a in range(HALVES)]

        ident = sb("ident", [P, P])
        upper = sb("upper", [P, P])
        ones = sb("ones", [P, P])
        iota_row = sb("iota_row", [P, P])
        iota_slot = sb("iota_slot", [P, CAP], BF16)
        token_id = sb("token_id", [P, TILES])
        token_id16 = sb("token_id16", [P, HALVES], BF16)
        half_power = sb("half_power", [P, NT * E])
        neg_half_power = sb("neg_half_power", [P, NT])
        gamma_c = sb("gamma_c", [P, 4])
        bias_b = sb("bias_b", [P, E])
        x_all = sb("x_all", [P, TILES, D])
        ctx_sb = sb("ctx_sb", [P, B, N])
        wq_sb = sb("wq_sb", [P, DC])
        wk_sb = sb("wk_sb", [P, DC])
        gate_sb = sb("gate_sb", [P, DK, E])
        w1_sb = [sb(f"w1_sb{r}", [P, DK, IP]) for r in range(3)]
        w3_sb = [sb(f"w3_sb{r}", [P, DK, IP]) for r in range(3)]
        w2_sb = [sb(f"w2_sb{r}", [P, MI, D]) for r in range(3)]
        q_sb = sb("q_sb", [P, N])
        k_sb = sb("k_sb", [P, N])
        sim = sb("sim", [P, NT, N])
        adj = sb("adj", [P, NT, N])
        junk = sb("junk", [P, NT, N], BF16)
        below = sb("below", [P, N])
        probe = sb("probe", [P, 2, NT])
        bracket = sb("bracket", [P, 2, 2, NT])
        is_low = sb("is_low", [P, NT], I32)
        is_high = sb("is_high", [P, NT], I32)
        step_a = sb("step_a", [P, NT])
        step_b = sb("step_b", [P, NT])
        need = sb("need", [P, NT])
        top8 = sb("top8", [P, NT, 8])
        pick8 = sb("pick8", [P, NT, 8])
        thr = sb("thr", [P, NT])
        open_rows = sb("open_rows", [P, NT])
        open_q = sb("open_q", [32, 32])
        open_t = sb("open_t", [32, 32])
        open_i = sb("open_i", [1, 1], I32)
        bn = sb("bn", [P, NT, 6])
        mv_x = sb("mv_x", [P, NT, 2])
        mv_s = sb("mv_s", [P, NT, 2])
        mv_y = sb("mv_y", [P, NT, 2])
        std_s = sb("std_s", [P, NT])
        ln_a = sb("ln_a", [P, NT])
        ln_mul = sb("ln_mul", [P, NT])
        ln_add = sb("ln_add", [P, NT])
        xn = sb("xn", [P, NT, D])
        xT = [sb(f"xT{r}", [P, DK, CAP]) for r in range(2)]
        logit = sb("logit", [P, NT, E])
        soft = sb("soft", [P, NT, E])
        score = sb("score", [P, NT, E])
        biased = sb("biased", [P, NT, E])
        best = sb("best", [P, NT, 8])
        best_i = sb("best_i", [P, NT, 8], U32)
        choice = sb("choice", [P, 2, NT])
        onehot = sb("onehot", [P, 2, NT, E])
        picked = sb("picked", [P, 2, NT, E])
        weight = sb("weight", [P, 2, NT])
        total = sb("total", [P, NT])
        mask = sb("mask", [P, NT, E])
        before = sb("before", [P, NT + 1, E])
        place = sb("place", [P, NT, E])
        slot = sb("slot", [P, 2, NT])
        upper_half = sb("upper_half", [P, 2, NT])
        column = sb("column", [P, 2, NT])
        spare = sb("spare", [P, HALVES, E], BF16)
        spare_hot = sb("spare_hot", [P, HALVES, E, CAP], BF16)
        row_hot = sb("row_hot", [P, 2 * NT, P])
        col_hot = sb("col_hot", [P, 2 * NT, 3, COLS])
        table = sb("table", [P, 3, COLS])
        spare_tab = sb("spare_tab", [P, COLS])
        slot_token = sb("slot_token", [P, COLS], I32)
        x_slots = [sb(f"x_slots{r}", [P, HALVES, D]) for r in range(2)]
        silu_g = sb("silu_g", [P, MI, CAP])
        up_u = sb("up_u", [P, MI, CAP])
        hidden = sb("hidden", [P, MI, CAP])
        y_sb = [sb(f"y_sb{r}", [P, HALVES, D]) for r in range(2)]

        wq_loaded, wk_loaded, small_loaded = sem("wq_loaded"), sem("wk_loaded"), sem("small_loaded")
        ctx_loaded = [sem(f"ctx_loaded{b}") for b in range(B)]
        x_loaded = [sem(f"x_loaded{b}") for b in range(B)]
        w13_loaded = [sem(f"w13_loaded{r}") for r in range(3)]
        w2_loaded = [sem(f"w2_loaded{r}") for r in range(3)]
        consts_ready = sem("consts_ready")
        pads_ready = sem("pads_ready")
        gamma_ready = sem("gamma_ready")
        filled = {n: sem(f"filled_{n}") for n in bank}
        drained = {n: sem(f"drained_{n}") for n in bank}
        qk_ready = sem("qk_ready")
        sim_ready, tanh_ready = sem("sim_ready"), sem("tanh_ready")
        sim_stats, std_ready = sem("sim_stats"), sem("std_ready")
        sig_ready, adj_ready, adj_added = sem("sig_ready"), sem("adj_ready"), sem("adj_added")
        x_stats, base_ready = sem("x_stats"), sem("base_ready")
        x1_stats, xn_ready, xn_stored = sem("x1_stats"), sem("xn_ready"), sem("xn_stored")
        soft_ready, score_ready = sem("soft_ready"), sem("score_ready")
        mask_ready, hot_ready, table_ready = sem("mask_ready"), sem("hot_ready"), sem("table_ready")
        logit_ready = sem("logit_ready")
        xT_ready, gu_ready, silu_ready, u_ready = sem("xT_ready"), sem("gu_ready"), sem("silu_ready"), sem("u_ready")
        h_ready, y_ready, y_copied, y_added = sem("h_ready"), sem("y_ready"), sem("y_copied"), sem("y_added")
        stored = [sem(f"stored{r}") for r in range(2)]
        gathered = [[sem(f"gathered{r}{a}") for a in range(HALVES)] for r in range(2)]
        scattered = sem("scattered")
        act_step, dve_step, pool_step = sem("act_step"), sem("dve_step"), sem("pool_step")

        block = ctx.enter_context(nc.Block())

        def load_expert(sp, w1, w3, w2, r):
            sp.dma_start(w1_sb[r][:, :, 0:I], w1).then_inc(w13_loaded[r], 16)
            sp.dma_start(w3_sb[r][:, :, 0:I], w3).then_inc(w13_loaded[r], 16)
            sp.dma_start(w2_sb[r][:, 0:MI - 1, :],
                         w2[0:(MI - 1) * P, :].rearrange("(c p) d -> p c d", p=P)).then_inc(w2_loaded[r], 16)
            sp.dma_start(w2_sb[r][0:LAST, MI - 1, :], w2[(MI - 1) * P:I, :]).then_inc(w2_loaded[r], 16)

        @block.sync
        def _(sp):
            sp.dma_start(ctx_sb[:, 0, :], ctxT[0]).then_inc(ctx_loaded[0], 16)
            sp.dma_start(wq_sb[:, :], WqT).then_inc(wq_loaded, 16)
            sp.dma_start(wk_sb[:, :], WkT).then_inc(wk_loaded, 16)
            sp.dma_start(gamma_c[:, 0:1], gamma_raw.partition_broadcast(P)).then_inc(small_loaded, 16)
            sp.dma_start(bias_b[:, :], gate_b.partition_broadcast(P)).then_inc(small_loaded, 16)
            sp.dma_start(gate_sb[:, :, :], gateT.rearrange("(c p) e -> p c e", p=P)).then_inc(small_loaded, 16)
            for b in range(B):
                if b:
                    sp.dma_start(ctx_sb[:, b, :], ctxT[b]).then_inc(ctx_loaded[b], 16)
                sp.dma_start(x_all[:, NT * b:NT * b + NT, :],
                             x[b].rearrange("(j p) d -> p j d", p=P)).then_inc(x_loaded[b], 16)
                if b == 0:
                    load_expert(sp, Ws1T, Ws3T, Ws2T, 2)
            for e in range(2):
                load_expert(sp, W1T[e], W3T[e], W2T[e], e)
            for b in range(B):
                sp.wait_ge(xn_ready, NT * (b + 1))
                sp.dma_start(xn_rows[N * b:N * b + N, :].rearrange("(j p) d -> p j d", p=P),
                             xn[:, :, :]).then_inc(xn_stored, 16)
                for n in (2 * b, 2 * b + 1):
                    sp.wait_ge(y_added, HALVES * (n + 1))
                    sp.dma_start(out_rows[CAP * n:CAP * n + CAP, :].rearrange("(a p) d -> p a d", p=P),
                                 y_sb[n % 2][:, :, :]).then_inc(stored[n % 2], 16)

            with sp.Fori(0, E // 2 - 1) as i:
                for r in range(2):
                    n = SHARED + 2 * i + r
                    e = 2 * i + 2 + r
                    sp.wait_ge(gu_ready, MI * n + MI)
                    sp.dma_start(w1_sb[r][:, :, 0:I], W1T[e]).then_inc(w13_loaded[r], 16)
                    sp.dma_start(w3_sb[r][:, :, 0:I], W3T[e]).then_inc(w13_loaded[r], 16)
                    sp.wait_ge(y_ready, HALVES * n + HALVES)
                    sp.dma_start(w2_sb[r][:, 0:MI - 1, :],
                                 W2T[e, 0:(MI - 1) * P, :].rearrange("(c p) d -> p c d", p=P)).then_inc(w2_loaded[r], 16)
                    sp.dma_start(w2_sb[r][0:LAST, MI - 1, :], W2T[e, (MI - 1) * P:I, :]).then_inc(w2_loaded[r], 16)
            sp.wait_ge(scattered, 16 * HALVES * E)
            sp.wait_ge(xn_stored, 16 * B)
            for r in range(2):
                sp.wait_ge(stored[r], 16 * (SHARED // 2))

        @block.tensor
        def _(pe):
            def take(name):
                which, k = turns[name]
                if k:
                    pe.wait_ge(drained[which], k)
                return bank[which], filled[which]

            def attention(b):
                pe.wait_ge(ctx_loaded[b], 16)
                if b == 0:
                    pe.wait_ge(wq_loaded, 16)
                dst, done = take(("q", b))
                nc.tensor.matmul(dst[:, :], wq_sb[:, :], ctx_sb[:, b, :], start=True, stop=True).then_inc(done, 1)
                if b == 0:
                    pe.wait_ge(wk_loaded, 16)
                dst, done = take(("k", b))
                nc.tensor.matmul(dst[:, :], wk_sb[:, :], ctx_sb[:, b, :], start=True, stop=True).then_inc(done, 1)
                pe.wait_ge(qk_ready, 2 * (b + 1))
                for j in range(NT):
                    dst, done = take(("sim", b, j))
                    nc.tensor.matmul(dst[:, :], q_sb[:, j * P:(j + 1) * P], k_sb[:, :],
                                     start=True, stop=True).then_inc(done, 1)

            def turn_adjacency(b):
                pe.wait_ge(adj_ready, NT * (b + 1))
                for i in range(NT):
                    dst, done = take(("adjT", b, i))
                    for j in range(NT):
                        last = nc.tensor.transpose(dst[:, j * P:(j + 1) * P], adj[:, j, i * P:(i + 1) * P], ident[:, :])
                    last.then_inc(done, 1)

            def turn_rows(dst, src):
                for c in range(DK):
                    last = nc.tensor.transpose(dst[:, c * P:(c + 1) * P], src[:, c * P:(c + 1) * P], ident[:, :])
                return last

            def batch_rows(b):
                for j in range(NT):
                    pe.wait_ge(xn_ready, NT * b + j + 1)
                    dst, done = take(("xT", b, j))
                    turn_rows(dst, xn[:, j, :]).then_inc(done, 1)

            def gate(b):
                if b == 0:
                    pe.wait_ge(small_loaded, 48)
                dst, done = take(("gate", b))
                for j in range(NT):
                    pe.wait_ge(xT_ready, NT * b + j + 1)
                    for c in range(DK):
                        last = nc.tensor.matmul(dst[:, j * E:(j + 1) * E],
                                                xT[j // 2][:, c, (j % 2) * P:(j % 2 + 1) * P], gate_sb[:, c, :],
                                                start=(c == 0), stop=(c == DK - 1))
                last.then_inc(done, 1)

            def places(b):
                pe.wait_ge(mask_ready, b + 1)
                dst, done = take(("place", b))
                nc.tensor.matmul(dst[:, 0:NT * E], upper[:, :], mask[:, :, :], start=True, stop=False)
                nc.tensor.matmul(dst[:, 0:NT * E], ones[:, :], before[:, 0:NT, :],
                                 start=False, stop=True).then_inc(done, 1)

            def slot_table(b):
                pe.wait_ge(hot_ready, b + 1)
                dst, done = take(("table", b))
                if b == 0:
                    for a in range(HALVES):
                        for e in range(E):
                            for h in range(HALVES):
                                at = (3 + a) * COLS + HALVES * e + h
                                nc.tensor.matmul(dst[:, at:at + 1], spare_hot[:, a, e, h * P:(h + 1) * P],
                                                 token_id16[:, a:a + 1], start=True, stop=True)
                for k in range(2 * NT):
                    last = nc.tensor.matmul(dst[:, 0:3 * COLS], row_hot[:, k, :], col_hot[:, k, :, :],
                                            start=(k == 0), stop=(k == 2 * NT - 1))
                last.then_inc(done, 1)

            def gate_up(n, r, s):
                pe.wait_ge(xT_ready, HALVES * n + HALVES)
                for m in range(MI):
                    for w, at in ((w1_sb[s], 0), (w3_sb[s], CAP)):
                        for c in range(DK):
                            last = nc.tensor.matmul(gu_bank[m][:, at:at + CAP], w[:, c, m * P:(m + 1) * P],
                                                    xT[r][:, c, :], start=(c == 0), stop=(c == DK - 1))
                    last.then_inc(gu_ready, 1)

            def down(n, s):
                for m in range(MI):
                    pe.wait_ge(h_ready, MI * n + m + 1)
                    rows = P if m < MI - 1 else LAST
                    for a in range(HALVES):
                        if m == 0:
                            if not isinstance(n, int) or n > 0:
                                pe.wait_ge(y_copied, HALVES * n - HALVES + a + 1)
                        last = nc.tensor.matmul(y_bank[a][:, :], hidden[0:rows, m, a * P:(a + 1) * P],
                                                w2_sb[s][0:rows, m, :], start=(m == 0), stop=(m == MI - 1))
                        if m == MI - 1:
                            last.then_inc(y_ready, 1)

            def expert_rows(n, r, count):
                for a in range(HALVES):
                    pe.wait_ge(gathered[r][a], 16 * count)
                    pe.wait_ge(drained[f"t{a}"], fills[f"t{a}"] + (n - SHARED))
                    turn_rows(bank[f"t{a}"], x_slots[r][:, a, :]).then_inc(filled[f"t{a}"], 1)

            def expert(i, r, more):
                n = SHARED + 2 * i + r
                pe.wait_ge(w13_loaded[r], 32 * i + 32)
                gate_up(n, r, r)
                if more:
                    expert_rows(n + 1, 1 - r, i + 1 + r)
                pe.wait_ge(w2_loaded[r], 32 * i + 32)
                down(n, r)

            pe.wait_ge(consts_ready, 1)
            attention(0)
            for b in range(B):
                turn_adjacency(b)
                if b + 1 < B:
                    attention(b + 1)
                batch_rows(b)
                gate(b)
                if b == 0:
                    pe.wait_ge(pads_ready, 1)
                    pe.wait_ge(w13_loaded[2], 32)
                gate_up(2 * b, 0, 2)
                if b == B - 1:
                    places(b)
                if b == 0:
                    pe.wait_ge(w2_loaded[2], 32)
                down(2 * b, 2)
                if b < B - 1:
                    places(b)
                else:
                    slot_table(b)
                gate_up(2 * b + 1, 1, 2)
                if b == B - 1:
                    expert_rows(SHARED, 0, 1)
                down(2 * b + 1, 2)
                if b < B - 1:
                    slot_table(b)
            with pe.Fori(0, E // 2 - 1) as i:
                expert(i, 0, True)
                expert(i, 1, True)
            expert(E // 2 - 1, 0, True)
            expert(E // 2 - 1, 1, False)

        @block.scalar
        def _(act):
            steps = Count()

            def chained(ins):
                ins.then_inc(act_step, 1)
                act.wait_ge(act_step, steps.up())

            def given(name):
                which, k = turns[name]
                act.wait_ge(filled[which], k + 1)
                return bank[which], drained[which]

            def attention(b):
                for name, dst, scale in (("q", q_sb, SIM_SCALE), ("k", k_sb, 1.0)):
                    src, free = given((name, b))
                    nc.scalar.activation(dst[:, :], src[:, :], ACT.Copy, scale=scale).then_inc(qk_ready, 1)
                    free_after(free)
                if b:
                    act.wait_ge(adj_added, NT * b)
                for j in range(NT):
                    src, free = given(("sim", b, j))
                    nc.scalar.activation(sim[:, j, :], src[:, :], ACT.Copy).then_inc(sim_ready, 1)
                    nc.scalar.activation(adj[:, j, :], src[:, :], ACT.Tanh, scale=0.5).then_inc(tanh_ready, 1)
                    free_after(free)

            def free_after(free):
                act.drain().then_inc(free, 1)

            def hidden_values(n):
                for m in range(MI):
                    act.wait_ge(gu_ready, MI * n + m + 1)
                    if n:
                        act.wait_ge(h_ready, MI * (n - 1) + m + 1)
                    nc.scalar.activation(silu_g[:, m, :], gu_bank[m][:, 0:CAP], ACT.Silu).then_inc(silu_ready, 1)
                    nc.scalar.activation(up_u[:, m, :], gu_bank[m][:, CAP:2 * CAP], ACT.Copy).then_inc(u_ready, 1)

            def result(n):
                for a in range(HALVES):
                    act.wait_ge(y_ready, HALVES * n + a + 1)
                    if n >= 2:
                        act.wait_ge(stored[n % 2], 16 * (n // 2))
                    nc.scalar.activation(y_sb[n % 2][:, a, :], y_bank[a][:, :], ACT.Copy).then_inc(y_copied, 1)

            act.wait_ge(small_loaded, 48)
            chained(nc.scalar.activation(gamma_c[:, 1:2], gamma_c[:, 0:1], ACT.Tanh, scale=0.5))
            nc.scalar.activation(gamma_c[:, 2:3], gamma_c[:, 1:2], ACT.Copy, scale=-0.5, bias=0.5)
            nc.scalar.activation(gamma_c[:, 3:4], gamma_c[:, 1:2], ACT.Copy, scale=0.125,
                                 bias=0.125).then_inc(gamma_ready, 1)
            attention(0)
            for b in range(B):
                if b + 1 < B:
                    attention(b + 1)
                for j in range(NT):
                    src, free = given(("xT", b, j))
                    dst = xT[j // 2][:, :, (j % 2) * P:(j % 2 + 1) * P]
                    if b:
                        act.wait_ge(gu_ready, MI * (2 * b - 2 + j // 2) + MI)
                    chained(nc.scalar.activation(dst, src[:, :].rearrange("p (c t) -> p c t", c=DK), ACT.Copy))
                    act.sem_inc(xT_ready, 1)
                    act.sem_inc(free, 1)
                src, free = given(("gate", b))
                if b:
                    act.wait_ge(mask_ready, b)
                chained(nc.scalar.activation(logit[:, :, :], src[:, 0:NT * E].rearrange("p (j e) -> p j e", j=NT),
                                             ACT.Copy))
                act.sem_inc(free, 1)
                act.sem_inc(logit_ready, 1)
                hidden_values(2 * b)
                chained(nc.scalar.activation(soft[:, :, :], logit[:, :, :], ACT.Abs))
                chained(nc.scalar.activation(soft[:, :, :], soft[:, :, :], ACT.Exp, scale=-1.0))
                nc.scalar.activation(soft[:, :, :], soft[:, :, :], ACT.Ln, bias=1.0).then_inc(soft_ready, 1)
                result(2 * b)
                hidden_values(2 * b + 1)
                result(2 * b + 1)

            act.wait_ge(table_ready, 1)

            def expert(i, r):
                n = SHARED + 2 * i + r
                for m in range(MI):
                    act.wait_ge(gu_ready, MI * n + m + 1)
                    nc.scalar.activation(silu_g[:, m, :], gu_bank[m][:, 0:CAP], ACT.Silu).then_inc(silu_ready, 1)
                if isinstance(i, int) and i == 0:
                    act.wait_ge(stored[r], 16 * (SHARED // 2))
                else:
                    act.wait_ge(scattered, 16 * HALVES * (2 * i + r - 1))
                for a in range(HALVES):
                    act.wait_ge(y_ready, HALVES * n + a + 1)
                    nc.scalar.activation(y_sb[r][:, a, :], y_bank[a][:, :], ACT.Copy,
                                         scale=table[:, 1, bass.ds(HALVES * (2 * i + r) + a, 1)]).then_inc(y_copied, 1)

            expert(0, 0)
            expert(0, 1)
            with act.Fori(1, E // 2) as i:
                expert(i, 0)
                expert(i, 1)

        @block.vector
        def _(dve):
            steps = Count()

            def chained(ins):
                ins.then_inc(dve_step, 1)
                dve.wait_ge(dve_step, steps.up())

            def given(name):
                which, k = turns[name]
                dve.wait_ge(filled[which], k + 1)
                return bank[which], drained[which]

            def stats(rows, mv, done):
                for j in range(NT):
                    last = nc.vector.bn_stats(bn[:, j, :], rows(j))
                chained(last)
                for j in range(NT):
                    last = nc.vector.bn_aggr(mv[:, j, :], bn[:, j, :])
                chained(last)
                dve.sem_inc(done, 1)

            def prepare(b):
                dve.wait_ge(sim_ready, NT * (b + 1))
                stats(lambda j: sim[:, j, 0:SAMPLE], mv_s, sim_stats)
                dve.wait_ge(x_loaded[b], 16)
                stats(lambda j: x_all[:, NT * b + j, :], mv_x, x_stats)

            def search(b):
                dve.wait_ge(std_ready, b + 1)
                for dst, z in ((probe[:, 0, :], Z_START), (bracket[:, 0, 0, :], Z_LOW), (bracket[:, 1, 0, :], Z_HIGH)):
                    nc.vector.scalar_tensor_tensor(out=dst, in0=std_s[:, :], scalar=z, in1=mv_s[:, :, 0],
                                                   op0=ALU.mult, op1=ALU.add)
                nc.vector.memset(bracket[:, 0, 1, :], COUNT_LOW)
                chained(nc.vector.memset(bracket[:, 1, 1, :], COUNT_HIGH))
                for k in range(SEARCH_STEPS):
                    for j in range(NT):
                        last = nc.vector.tensor_scalar(junk[:, j, :], sim[:, j, :], probe[:, 0, j:j + 1], None,
                                                       ALU.is_ge, ALU.add, accum_out=probe[:, 1, j:j + 1])
                    chained(last)
                    nc.vector.tensor_scalar(is_low[:, :], probe[:, 1, :], float(KTH), None, ALU.is_ge)
                    chained(nc.vector.tensor_scalar(is_high[:, :], probe[:, 1, :], float(KTH), None, ALU.is_lt))
                    for side, m in ((0, is_low), (1, is_high)):
                        last = nc.vector.copy_predicated(bracket[:, side, :, :],
                                                         m[:, :].unsqueeze(1).to_broadcast([P, 2, NT]), probe[:, :, :])
                    chained(last)
                    if k == SEARCH_STEPS - 1:
                        break
                    low, high = bracket[:, 0], bracket[:, 1]
                    chained(nc.vector.tensor_tensor(step_a[:, :], low[:, 1, :], high[:, 1, :], ALU.subtract))
                    chained(nc.vector.reciprocal(step_b[:, :], step_a[:, :]))
                    nc.vector.tensor_tensor(step_a[:, :], high[:, 0, :], low[:, 0, :], ALU.subtract)
                    chained(nc.vector.scalar_tensor_tensor(out=step_b[:, :], in0=low[:, 1, :], scalar=COUNT_AIM,
                                                           in1=step_b[:, :], op0=ALU.subtract, op1=ALU.mult))
                    chained(nc.vector.scalar_tensor_tensor(out=step_b[:, :], in0=step_b[:, :], scalar=1.0,
                                                           in1=step_a[:, :], op0=ALU.min, op1=ALU.mult))
                    chained(nc.vector.tensor_tensor(probe[:, 0, :], step_b[:, :], low[:, 0, :], ALU.add))

            def threshold(b):
                high_t, high_count = bracket[:, 1, 0, :], bracket[:, 1, 1, :]
                nc.vector.tensor_scalar(need[:, :], high_count, -1.0, float(KTH - 1), ALU.mult, ALU.add)
                for j in range(NT):
                    chained(nc.vector.tensor_scalar(below[:, :], sim[:, j, :], high_t[:, j:j + 1], -BIG,
                                                    ALU.is_ge, ALU.mult))
                    chained(nc.vector.tensor_tensor(below[:, :], below[:, :], sim[:, j, :], ALU.add))
                    chained(nc.vector.max(top8[:, j, :], below[:, :]))
                chained(nc.vector.tensor_tensor(pick8[:, :, :],
                                                iota_row[:, 0:8].unsqueeze(1).to_broadcast([P, NT, 8]),
                                                need[:, :].unsqueeze(2).to_broadcast([P, NT, 8]), ALU.is_equal))
                chained(nc.vector.tensor_tensor(pick8[:, :, :], pick8[:, :, :], top8[:, :, :], ALU.mult))
                chained(nc.vector.tensor_reduce(thr[:, :], pick8[:, :, :], AX_X, ALU.add))
                chained(nc.vector.tensor_scalar(open_rows[:, :], need[:, :], 7.5, None, ALU.is_ge, ALU.add,
                                                accum_out=step_a[:, 0:1]))
                chained(nc.vector.memset(open_q[:, :], 0.0))
                for q in range(4):
                    last = nc.vector.tensor_copy(open_q[:, q:q + 1], step_a[32 * q:32 * q + 32, 0:1])
                chained(last)
                chained(nc.vector.transpose(open_t[:, :], open_q[:, :]))
                chained(nc.vector.tensor_reduce(open_q[:, 0:1], open_t[:, :], AX_X, ALU.max))
                chained(nc.vector.transpose(open_t[:, :], open_q[:, :]))
                chained(nc.vector.tensor_reduce(open_q[0:1, 0:1], open_t[0:1, 0:4], AX_X, ALU.max))
                chained(nc.vector.tensor_copy(open_i[:, :], open_q[0:1, 0:1]))
                rows_open = dve.value_load(open_i[0:1, 0:1], min_val=0, max_val=NT)
                with dve.If(rows_open > 0):
                    for j in range(NT):
                        nc.vector.tensor_copy(below[:, :], sim[:, j, :])
                        dve.drain()
                        with dve.Fori(0, (KTH - 1) // 8):
                            nc.vector.max(top8[:, j, :], below[:, :])
                            dve.drain()
                            nc.vector.match_replace(below[:, :], top8[:, j, :], below[:, :], -BIG)
                            dve.drain()
                        nc.vector.max(top8[:, j, :], below[:, :])
                        dve.drain()
                        nc.vector.tensor_copy(thr[:, j:j + 1], top8[:, j, (KTH - 1) % 8:(KTH - 1) % 8 + 1])
                        dve.drain()

            def adjacency(b):
                dve.wait_ge(sig_ready, b + 1)
                for j in range(NT):
                    nc.vector.scalar_tensor_tensor(out=adj[:, j, :], in0=sim[:, j, :], scalar=thr[:, j:j + 1],
                                                   in1=adj[:, j, :], op0=ALU.is_ge, op1=ALU.mult).then_inc(adj_ready, 1)
                dve.wait_ge(adj_ready, NT * (b + 1))
                dve.wait_ge(base_ready, b + 1)
                for j in range(NT):
                    t = NT * b + j
                    nc.vector.tensor_tensor(x_all[:, t, :], x_all[:, t, :], adj[:, j, :],
                                            ALU.add).then_inc(adj_added, 1)

            def residual(b):
                dve.wait_ge(adj_added, NT * (b + 1))
                for j in range(NT):
                    t = NT * b + j
                    src, free = given(("adjT", b, j))
                    chained(nc.vector.tensor_tensor(x_all[:, t, :], x_all[:, t, :], src[:, :], ALU.add))
                    dve.sem_inc(free, 1)
                stats(lambda j: x_all[:, NT * b + j, :], mv_y, x1_stats)

            def choose(b):
                dve.wait_ge(score_ready, b + 1)
                chained(nc.vector.tensor_tensor(biased[:, :, :], score[:, :, :],
                                                bias_b[:, :].unsqueeze(1).to_broadcast([P, NT, E]), ALU.add))
                for j in range(NT):
                    last = nc.vector.max(best[:, j, :], biased[:, j, :])
                chained(last)
                for j in range(NT):
                    last = nc.vector.max_index(best_i[:, j, :], best[:, j, :], biased[:, j, :])
                chained(last)
                chained(nc.vector.tensor_copy(choice[:, :, :], best_i[:, :, 0:2].rearrange("p j k -> p k j")))
                for k in range(2):
                    last = nc.vector.tensor_tensor(onehot[:, k, :, :],
                                                   iota_row[:, 0:E].unsqueeze(1).to_broadcast([P, NT, E]),
                                                   choice[:, k, :].unsqueeze(2).to_broadcast([P, NT, E]), ALU.is_equal)
                chained(last)
                for k in range(2):
                    nc.vector.tensor_tensor(picked[:, k, :, :], onehot[:, k, :, :], score[:, :, :], ALU.mult)
                chained(nc.vector.tensor_tensor(mask[:, :, :], onehot[:, 0, :, :], onehot[:, 1, :, :], ALU.add))
                if b:
                    chained(nc.vector.tensor_copy(before[:, 0, :], before[:, NT, :]))
                for j in range(NT):
                    chained(nc.vector.tensor_tensor(before[:, j + 1, :], before[:, j, :], mask[:, j, :], ALU.add))
                dve.sem_inc(mask_ready, 1)
                chained(nc.vector.tensor_reduce(weight[:, :, :], picked[:, :, :, :], AX_X, ALU.add))
                chained(nc.vector.tensor_tensor(total[:, :], weight[:, 0, :], weight[:, 1, :], ALU.add))
                chained(nc.vector.reciprocal(total[:, :], total[:, :]))
                for k in range(2):
                    last = nc.vector.tensor_tensor(weight[:, k, :], weight[:, k, :], total[:, :], ALU.mult)
                chained(last)

            def place_tokens(b):
                src, free = given(("place", b))
                chained(nc.vector.tensor_copy(place[:, :, :], src[:, 0:NT * E].rearrange("p (j e) -> p j e", j=NT)))
                dve.sem_inc(free, 1)
                for k in range(2):
                    last = nc.vector.tensor_tensor(picked[:, k, :, :], onehot[:, k, :, :], place[:, :, :], ALU.mult)
                chained(last)
                chained(nc.vector.tensor_reduce(slot[:, :, :], picked[:, :, :, :], AX_X, ALU.add))
                chained(nc.vector.tensor_scalar(upper_half[:, :, :], slot[:, :, :], float(P), None, ALU.is_ge))
                chained(nc.vector.scalar_tensor_tensor(out=slot[:, :, :], in0=upper_half[:, :, :], scalar=-float(P),
                                                       in1=slot[:, :, :], op0=ALU.mult, op1=ALU.add))
                chained(nc.vector.scalar_tensor_tensor(out=column[:, :, :], in0=choice[:, :, :], scalar=float(HALVES),
                                                       in1=upper_half[:, :, :], op0=ALU.mult, op1=ALU.add))
                for j in range(NT):
                    t = NT * b + j
                    for k in range(2):
                        at = 2 * j + k
                        nc.vector.tensor_scalar(row_hot[:, at, :], iota_row[:, :], slot[:, k, j:j + 1], None,
                                                ALU.is_equal)
                        nc.vector.tensor_scalar(col_hot[:, at, 0, :], iota_row[:, 0:COLS], column[:, k, j:j + 1],
                                                token_id[:, t:t + 1], ALU.is_equal, ALU.mult)
                        nc.vector.tensor_scalar(col_hot[:, at, 1, :], iota_row[:, 0:COLS], column[:, k, j:j + 1],
                                                weight[:, k, j:j + 1], ALU.is_equal, ALU.mult)
                        last = nc.vector.tensor_scalar(col_hot[:, at, 2, :], iota_row[:, 0:COLS],
                                                       column[:, k, j:j + 1], None, ALU.is_equal)
                if b == 0:
                    for a in range(HALVES):
                        chained(nc.vector.tensor_scalar(spare[:, a, :], place[:, a, :], token_id[:, a:a + 1],
                                                        float(CAP - 1), ALU.subtract, ALU.add))
                        chained(nc.vector.scalar_tensor_tensor(out=spare[:, a, :], in0=mask[:, a, :],
                                                               scalar=float(2 * CAP), in1=spare[:, a, :],
                                                               op0=ALU.mult, op1=ALU.add))
                        last = nc.vector.tensor_tensor(spare_hot[:, a, :, :],
                                                       iota_slot[:, :].unsqueeze(1).to_broadcast([P, E, CAP]),
                                                       spare[:, a, :].unsqueeze(2).to_broadcast([P, E, CAP]),
                                                       ALU.is_equal)
                chained(last)
                dve.sem_inc(hot_ready, 1)

            def add_table(b):
                src, free = given(("table", b))
                got = src[:, 0:3 * COLS].rearrange("p (v c) -> p v c", v=3)
                if b == 0:
                    nc.vector.tensor_copy(table[:, :, :], got)
                    chained(nc.vector.tensor_copy(spare_tab[:, :], src[:, 3 * COLS:4 * COLS]))
                    chained(nc.vector.tensor_tensor(spare_tab[:, :], spare_tab[:, :], src[:, 4 * COLS:5 * COLS], ALU.add))
                else:
                    chained(nc.vector.tensor_tensor(table[:, :, :], table[:, :, :], got, ALU.add))
                dve.sem_inc(free, 1)

            nc.vector.memset(before[:, 0, :], 0.0)
            prepare(0)
            for b in range(B):
                search(b)
                if b:
                    choose(b - 1)
                threshold(b)
                if b:
                    place_tokens(b - 1)
                adjacency(b)
                if b:
                    add_table(b - 1)
                residual(b)
                if b + 1 < B:
                    prepare(b + 1)
            choose(B - 1)
            place_tokens(B - 1)
            add_table(B - 1)
            chained(nc.vector.tensor_scalar(table[:, 2, :], table[:, 2, :], -1.0, 1.0, ALU.mult, ALU.add))
            chained(nc.vector.tensor_tensor(spare_tab[:, :], spare_tab[:, :], table[:, 2, :], ALU.mult))
            nc.vector.tensor_tensor(slot_token[:, :], spare_tab[:, :], table[:, 0, :], ALU.add).then_inc(table_ready, 1)

            def turned_rows(n, r):
                for a in range(HALVES):
                    dve.wait_ge(filled[f"t{a}"], fills[f"t{a}"] + (n - SHARED) + 1)
                    nc.vector.tensor_copy(xT[r][:, :, a * P:(a + 1) * P],
                                          bank[f"t{a}"][:, :].rearrange("p (c t) -> p c t", c=DK)).then_inc(xT_ready, 1)
                    dve.drain().then_inc(drained[f"t{a}"], 1)

            def expert(i, r, more):
                n = SHARED + 2 * i + r
                for m in range(MI):
                    dve.wait_ge(silu_ready, MI * n + m + 1)
                    nc.vector.tensor_tensor(hidden[:, m, :], silu_g[:, m, :], gu_bank[m][:, CAP:2 * CAP],
                                            ALU.mult).then_inc(h_ready, 1)
                if more:
                    turned_rows(n + 1, 1 - r)

            turned_rows(SHARED, 0)
            with dve.Fori(0, E // 2 - 1) as i:
                expert(i, 0, True)
                expert(i, 1, True)
            expert(E // 2 - 1, 0, True)
            expert(E // 2 - 1, 1, False)

        @block.gpsimd
        def _(pool):
            steps = Count()

            def chained(ins):
                ins.then_inc(pool_step, 1)
                pool.wait_ge(pool_step, steps.up())

            chained(nc.gpsimd.memset(ones[:, :], 1.0))
            chained(nc.gpsimd.affine_select(out=ident[:, :], in_=ones[:, :], compare_op=ALU.is_equal, fill=0.0,
                                            base=0, pattern=[[1, P]], channel_multiplier=-1))
            chained(nc.gpsimd.affine_select(out=upper[:, :], in_=ones[:, :], compare_op=ALU.is_gt, fill=0.0,
                                            base=0, pattern=[[1, P]], channel_multiplier=-1))
            nc.gpsimd.memset(half_power[:, :], 0.5)
            nc.gpsimd.memset(neg_half_power[:, :], -0.5)
            nc.gpsimd.iota(iota_row[:, :], pattern=[[1, P]], base=0, channel_multiplier=0,
                           allow_small_or_imprecise_dtypes=True)
            nc.gpsimd.iota(iota_slot[:, :], pattern=[[1, CAP]], base=0, channel_multiplier=0,
                           allow_small_or_imprecise_dtypes=True)
            nc.gpsimd.iota(token_id16[:, :], pattern=[[P, HALVES]], base=0, channel_multiplier=1,
                           allow_small_or_imprecise_dtypes=True)
            chained(nc.gpsimd.iota(token_id[:, :], pattern=[[P, TILES]], base=0, channel_multiplier=1,
                                   allow_small_or_imprecise_dtypes=True))
            pool.sem_inc(consts_ready, 1)
            for r in range(3):
                for w in (w1_sb[r], w3_sb[r]):
                    last = nc.gpsimd.memset(w[:, :, I:IP], 0.0)
            last.then_inc(pads_ready, 1)

            def spread(b):
                pool.wait_ge(sim_stats, b + 1)
                nc.gpsimd.tensor_tensor(std_s[:, :], mv_s[:, :, 1], half_power[:, 0:NT], ALU.pow).then_inc(std_ready, 1)

            def sigmoids(b):
                if b == 0:
                    pool.wait_ge(gamma_ready, 1)
                pool.wait_ge(tanh_ready, NT * (b + 1))
                nc.gpsimd.tensor_scalar(adj[:, :, :], adj[:, :, :], 1.0, gamma_c[:, 3:4],
                                        ALU.add, ALU.mult).then_inc(sig_ready, 1)

            def rstd(mv):
                chained(nc.gpsimd.tensor_scalar(ln_a[:, :], mv[:, :, 1], EPS, 1.0, ALU.add, ALU.mult))
                chained(nc.gpsimd.tensor_tensor(ln_a[:, :], ln_a[:, :], neg_half_power[:, :], ALU.pow))

            def base(b):
                pool.wait_ge(x_stats, b + 1)
                rstd(mv_x)
                chained(nc.gpsimd.tensor_scalar(ln_a[:, :], ln_a[:, :], gamma_c[:, 2:3], -1.0, ALU.mult, ALU.mult))
                chained(nc.gpsimd.tensor_tensor(ln_add[:, :], mv_x[:, :, 0], ln_a[:, :], ALU.mult))
                chained(nc.gpsimd.tensor_scalar(ln_mul[:, :], ln_a[:, :], -1.0, 1.0, ALU.mult, ALU.add))
                for j in range(NT):
                    t = NT * b + j
                    last = nc.gpsimd.tensor_scalar(x_all[:, t, :], x_all[:, t, :], ln_mul[:, j:j + 1],
                                                   ln_add[:, j:j + 1], ALU.mult, ALU.add)
                chained(last)
                pool.sem_inc(base_ready, 1)

            def normed(b):
                pool.wait_ge(x1_stats, b + 1)
                if b:
                    pool.wait_ge(xn_stored, 16 * b)
                rstd(mv_y)
                chained(nc.gpsimd.tensor_tensor(ln_add[:, :], mv_y[:, :, 0], ln_a[:, :], ALU.mult))
                chained(nc.gpsimd.tensor_scalar(ln_add[:, :], ln_add[:, :], -1.0, 0.0, ALU.mult, ALU.add))
                for j in range(NT):
                    nc.gpsimd.tensor_scalar(xn[:, j, :], x_all[:, NT * b + j, :], ln_a[:, j:j + 1],
                                            ln_add[:, j:j + 1], ALU.mult, ALU.add).then_inc(xn_ready, 1)
                pool.wait_ge(xn_ready, NT * (b + 1))

            def scores(b):
                pool.wait_ge(soft_ready, b + 1)
                if b:
                    pool.wait_ge(mask_ready, b)
                chained(nc.gpsimd.tensor_scalar(score[:, :, :], logit[:, :, :], 0.0, 0.0, ALU.max, ALU.add))
                chained(nc.gpsimd.tensor_tensor(score[:, :, :], score[:, :, :], soft[:, :, :], ALU.add))
                chained(nc.gpsimd.tensor_tensor(score[:, :, :], score[:, :, :],
                                                half_power[:, :].rearrange("p (j e) -> p j e", j=NT), ALU.pow))
                pool.sem_inc(score_ready, 1)

            def hidden_values(n):
                for m in range(MI):
                    pool.wait_ge(u_ready, MI * n + m + 1)
                    pool.wait_ge(silu_ready, MI * n + m + 1)
                    nc.gpsimd.tensor_tensor(hidden[:, m, :], silu_g[:, m, :], up_u[:, m, :],
                                            ALU.mult).then_inc(h_ready, 1)

            def add_residual(n):
                for a in range(HALVES):
                    pool.wait_ge(y_copied, HALVES * n + a + 1)
                    nc.gpsimd.tensor_tensor(y_sb[n % 2][:, a, :], y_sb[n % 2][:, a, :], x_all[:, HALVES * n + a, :],
                                            ALU.add).then_inc(y_added, 1)

            def gather(e):
                r = e % 2
                for a in range(HALVES):
                    if e >= 2:
                        pool.wait_ge(filled[f"t{a}"], fills[f"t{a}"] + e - 1)
                    at = HALVES * e + a
                    nc.gpsimd.indirect_dma_start(
                        out=x_slots[r][:, a, :], out_offset=None, in_=xn_rows[:, :],
                        in_offset=bass.IndirectOffsetOnAxis(ap=slot_token[:, at:at + 1], axis=0),
                    ).then_inc(gathered[r][a], 16)

            def scatter(e):
                for a in range(HALVES):
                    at = HALVES * e + a
                    pool.wait_ge(y_copied, HALVES * (SHARED + e) + a + 1)
                    if at:
                        pool.wait_ge(scattered, 16 * at)
                    nc.gpsimd.indirect_dma_start(
                        out=out_rows[:, :], out_offset=bass.IndirectOffsetOnAxis(ap=slot_token[:, at:at + 1], axis=0),
                        in_=y_sb[e % 2][:, a, :], in_offset=None, compute_op=ALU.add,
                    ).then_inc(scattered, 16)

            spread(0)
            sigmoids(0)
            base(0)
            for b in range(B):
                normed(b)
                more = b + 1 < B
                if more:
                    spread(b + 1)
                hidden_values(2 * b)
                if more:
                    sigmoids(b + 1)
                scores(b)
                add_residual(2 * b)
                if more:
                    base(b + 1)
                hidden_values(2 * b + 1)
                if not more:
                    pool.wait_ge(table_ready, 1)
                    pool.wait_ge(xn_stored, 16 * B)
                    gather(0)
                    gather(1)
                add_residual(2 * b + 1)

            for r in range(2):
                pool.wait_ge(stored[r], 16 * (SHARED // 2))
            for e in range(E):
                if e + 2 < E:
                    gather(e + 2)
                scatter(e)


_OUT = (4, 512, 512)


def kernel(x, ctx_512, L0_xattn_Wq, L0_xattn_Wk, L0_xattn_gamma_raw, L0_ffn_input_ids, L0_ffn_gate_w, L0_ffn_gate_b,
           L0_ffn_W1, L0_ffn_W3, L0_ffn_W2, L0_ffn_Ws1, L0_ffn_Ws3, L0_ffn_Ws2):
    import concourse.bacc as _bacc
    from concourse.bass_utils import run_bass_kernel_spmd as _run

    def by_rows(w):
        w = np.swapaxes(np.asarray(w), -1, -2)
        w = w.reshape(w.shape[:-2] + (w.shape[-2] // P, P, w.shape[-1]))
        return np.swapaxes(w, -3, -2)

    laid = {
        "x": np.asarray(x),
        "ctxT": np.swapaxes(np.asarray(ctx_512), 1, 2),
        "WqT": np.asarray(L0_xattn_Wq).T,
        "WkT": np.asarray(L0_xattn_Wk).T,
        "gamma_raw": np.asarray(L0_xattn_gamma_raw).reshape(1),
        "gateT": np.asarray(L0_ffn_gate_w).T,
        "gate_b": np.asarray(L0_ffn_gate_b),
        "W1T": by_rows(L0_ffn_W1),
        "W3T": by_rows(L0_ffn_W3),
        "W2T": np.swapaxes(np.asarray(L0_ffn_W2), 1, 2),
        "Ws1T": by_rows(L0_ffn_Ws1),
        "Ws3T": by_rows(L0_ffn_Ws3),
        "Ws2T": np.asarray(L0_ffn_Ws2).T,
    }
    nc = _bacc.Bacc("TRN2", target_bir_lowering=False, num_devices=1)
    arrays, args = {}, []
    for name, a in laid.items():
        a = np.ascontiguousarray(a)
        arrays[f"in_{name}"] = a
        args.append(nc.dram_tensor(f"in_{name}", a.shape, mybir.dt.from_np(a.dtype), kind="ExternalInput").ap())
    args.append(nc.dram_tensor("out_0", _OUT, F32, kind="ExternalOutput").ap())
    build(nc, *args)
    r = _run(nc, [arrays], core_ids=[0])
    return r.results[0]["out_0"]
```

```python
from contextlib import ExitStack

import numpy as np
import concourse.bass as bass
from concourse import mybir

ALU = mybir.AluOpType
ACT = mybir.ActivationFunctionType
AX_X = mybir.AxisListType.X
F32 = mybir.dt.float32
F32R = mybir.dt.float32r
BF16 = mybir.dt.bfloat16
I32 = mybir.dt.int32
U32 = mybir.dt.uint32

P = 128
EPS = 1e-5
HEADS = 4
TOP_K_RATIO = 0.3
CAP = 256
SEARCH_STEPS = 5
BIG = 1e30


class Count:

    def __init__(self):
        self.value = 0

    def up(self, n=1):
        self.value += n
        return self.value


def bank_turns(batches):
    order = []

    def attn(b):
        order.extend([("t0", ("q", b)), ("t1", ("k", b))])
        order.extend((f"t{j % 2}", ("sim", b, j)) for j in range(4))

    attn(0)
    for b in range(batches):
        order.extend((f"t{j % 2}", ("adjT", b, j)) for j in range(4))
        if b + 1 < batches:
            attn(b + 1)
        order.extend((f"t{j % 2}", ("xT", b, j)) for j in range(4))
        order.extend([("s", ("gate", b)), ("s", ("place", b)), ("s", ("table", b))])
    seen, turns = {}, {}
    for bank, name in order:
        turns[name] = (bank, seen.get(bank, 0))
        seen[bank] = seen.get(bank, 0) + 1
    return turns, seen


def build(nc, x, ctxT, WqT, WkT, gamma_raw, gateT, gate_b, W1T, W3T, W2T, Ws1T, Ws3T, Ws2T, out):
    B, N, D = x.shape
    DC = ctxT.shape[1]
    E, _, DK, I = W1T.shape
    T = B * N
    NT = N // P
    TILES = T // P
    MI = -(-I // P)
    LAST = I - (MI - 1) * P
    HALVES = CAP // P
    COLS = E * HALVES
    KTH = max(1, int(N * TOP_K_RATIO))
    SHARED = T // CAP
    SIM_SCALE = 1.0 / (float(np.sqrt(np.float32(DC // HEADS))) * HEADS)
    Z_START, Z_LOW, Z_HIGH = 0.52, -0.3, 1.3
    COUNT_LOW, COUNT_HIGH, COUNT_AIM = 0.618 * N, 0.097 * N, KTH - 4.0
    BY_DVE = NT // 2
    SAMPLE = N // 2
    assert DC == P and DK == D // P and T % CAP == 0 and HALVES == 2 and NT == 4 and D == N == 512

    x_rows = x.rearrange("b n d -> (b n) d")
    out_rows = out.rearrange("b n d -> (b n) d")
    xn_rows = nc.dram_tensor("xn_rows", [T, D], F32).ap()
    turns, fills = bank_turns(B)

    with ExitStack() as ctx:
        def sb(name, shape, dt=F32):
            return ctx.enter_context(nc.sbuf_tensor(name, shape, dt))

        def sem(name):
            return ctx.enter_context(nc.semaphore(name))

        bank = {n: ctx.enter_context(nc.psum_tensor(f"bank_{n}", [P, 512], F32)) for n in ("t0", "t1", "s")}
        gu_bank = [ctx.enter_context(nc.psum_tensor(f"gu_bank{m}", [P, 512], F32)) for m in range(MI)]
        y_bank = [ctx.enter_context(nc.psum_tensor(f"y_bank{a}", [P, D], F32)) for a in range(HALVES)]

        ident = sb("ident", [P, P])
        upper = sb("upper", [P, P])
        ones = sb("ones", [P, P])
        iota_row = sb("iota_row", [P, P])
        iota_slot = sb("iota_slot", [P, CAP], BF16)
        token_id = sb("token_id", [P, TILES])
        token_id16 = sb("token_id16", [P, HALVES], BF16)
        half_power = sb("half_power", [P, NT])
        neg_half_power = sb("neg_half_power", [P, NT])
        gamma_c = sb("gamma_c", [P, 4])
        bias_b = sb("bias_b", [P, E])
        x_sb = sb("x_sb", [P, 2 * NT, D])
        ctx_sb = sb("ctx_sb", [P, 2, N])
        wq_sb = sb("wq_sb", [P, DC])
        wk_sb = sb("wk_sb", [P, DC])
        gate_sb = sb("gate_sb", [P, DK, E])
        w1_raw = sb("w1_raw", [P, DK, I])
        w3_raw = sb("w3_raw", [P, DK, I])
        w2_raw = sb("w2_raw", [P, MI, D])
        base_0 = nc.sbuf_base
        spare_hot = nc.alloc_sbuf_tensor_at("spare_hot", [P, HALVES, E, CAP], BF16, offset=base_0)
        w1_hi, w1_lo, w3_hi, w3_lo, w2_hi, w2_lo = [], [], [], [], [], []
        for r in range(2):
            for name, shape, parts in (("w1", [P, DK, I], (w1_hi, w1_lo)), ("w3", [P, DK, I], (w3_hi, w3_lo)),
                                       ("w2", [P, MI, D], (w2_hi, w2_lo))):
                for part, kept in zip(("hi", "lo"), parts):
                    kept.append(sb(f"{name}_{part}{r}", shape, F32R))
        q_sb = sb("q_sb", [P, N])
        k_sb = sb("k_sb", [P, N])
        sim = sb("sim", [P, NT, N])
        adj = sb("adj", [P, NT, N])
        above = sb("above", [P, NT, N], BF16)
        signs = sb("signs", [P, NT, N], BF16)
        below = [sb(f"below{r}", [P, N]) for r in range(2)]
        probe = sb("probe", [P, 2, NT])
        bracket = sb("bracket", [P, 2, 2, NT])
        is_low = sb("is_low", [P, NT], I32)
        is_high = sb("is_high", [P, NT], I32)
        step_a = sb("step_a", [P, NT])
        step_b = sb("step_b", [P, NT])
        step_c = sb("step_c", [P, NT])
        exact = sb("exact", [P, NT])
        need = sb("need", [P, NT])
        top8 = sb("top8", [P, NT, 8])
        pick8 = sb("pick8", [P, NT, 8])
        thr = sb("thr", [P, NT])
        open_rows = sb("open_rows", [P, NT])
        open_q = sb("open_q", [32, 32])
        open_t = sb("open_t", [32, 32])
        open_i = sb("open_i", [1, 1], I32)
        bn = sb("bn", [P, NT, 6])
        x_moment = sb("x_moment", [P, 2, NT])
        x_var = sb("x_var", [P, NT])
        mv_s = sb("mv_s", [P, NT, 2])
        mv_y = sb("mv_y", [P, NT, 2])
        std_s = sb("std_s", [P, NT])
        ln_a = sb("ln_a", [P, NT])
        ln_mul = sb("ln_mul", [P, NT])
        ln_add = sb("ln_add", [P, NT])
        xn = sb("xn", [P, NT, D])
        xT_hi = [sb(f"xT_hi{r}", [P, DK, CAP], F32R) for r in range(2)]
        xT_lo = [sb(f"xT_lo{r}", [P, DK, CAP], F32R) for r in range(2)]
        logit = sb("logit", [P, NT, E])
        soft = sb("soft", [P, NT, E])
        rough = sb("rough", [P, NT, E])
        score = sb("score", [P, NT, E])
        biased = sb("biased", [P, NT, E])
        best = sb("best", [P, NT, 8])
        best_i = sb("best_i", [P, NT, 8], U32)
        choice = sb("choice", [P, 2, NT])
        onehot = sb("onehot", [P, 2, NT, E])
        picked = sb("picked", [P, 2, NT, E])
        weight = sb("weight", [P, 2, NT])
        total = sb("total", [P, NT])
        mask = sb("mask", [P, NT, E])
        before = sb("before", [P, NT + 1, E])
        place = sb("place", [P, NT, E])
        slot = sb("slot", [P, 2, NT])
        upper_half = sb("upper_half", [P, 2, NT])
        column = sb("column", [P, 2, NT])
        spare = sb("spare", [P, HALVES, E])
        row_hot = sb("row_hot", [P, 2, NT, P])
        col_hot = sb("col_hot", [P, 3, 2, NT, COLS])
        table = sb("table", [P, 3, COLS])
        spare_tab = sb("spare_tab", [P, COLS])
        slot_token = sb("slot_token", [P, COLS], I32)
        x_slots = [xn[:, HALVES * r:HALVES * r + HALVES, :] for r in range(2)]
        silu_g = sb("silu_g", [P, MI, CAP])
        up_u = sb("up_u", [P, MI, CAP])
        hidden = sb("hidden", [P, MI, CAP])
        hidden_hi = sb("hidden_hi", [P, MI, CAP], F32R)
        hidden_lo = sb("hidden_lo", [P, MI, CAP], F32R)
        y_sb = [sb(f"y_sb{r}", [P, HALVES, D]) for r in range(2)]

        wq_loaded, wk_loaded, small_loaded = sem("wq_loaded"), sem("wk_loaded"), sem("small_loaded")
        ctx_loaded = [sem(f"ctx_loaded{b}") for b in range(B)]
        x_loaded = [sem(f"x_loaded{b}") for b in range(B)]
        w1_loaded, w3_loaded, w2_loaded = sem("w1_loaded"), sem("w3_loaded"), sem("w2_loaded")
        shared_hi_ready, shared_split = sem("shared_hi_ready"), sem("shared_split")
        w_hi_ready, w_split = sem("w_hi_ready"), sem("w_split")
        consts_ready = sem("consts_ready")
        pads_ready = sem("pads_ready")
        gamma_ready = sem("gamma_ready")
        filled = {n: sem(f"filled_{n}") for n in bank}
        drained = {n: sem(f"drained_{n}") for n in bank}
        qk_ready = sem("qk_ready")
        sim_ready, tanh_ready = sem("sim_ready"), sem("tanh_ready")
        sim_stats, std_ready = sem("sim_stats"), sem("std_ready")
        sig_ready, adj_ready, adj_added = sem("sig_ready"), sem("adj_ready"), sem("adj_added")
        probe_ready, signs_ready = sem("probe_ready"), sem("signs_ready")
        x_stats = sem("x_stats")
        x1_stats, xn_ready, xn_stored = sem("x1_stats"), sem("xn_ready"), sem("xn_stored")
        soft_ready, score_ready, rough_ready = sem("soft_ready"), sem("score_ready"), sem("rough_ready")
        mask_ready, hot_ready, table_ready = sem("mask_ready"), sem("hot_ready"), sem("table_ready")
        logit_ready = sem("logit_ready")
        xT_hi_ready, xT_ready = sem("xT_hi_ready"), sem("xT_ready")
        gu_ready, silu_ready, u_ready = sem("gu_ready"), sem("silu_ready"), sem("u_ready")
        h_ready, h_hi_ready, h_split = sem("h_ready"), sem("h_hi_ready"), sem("h_split")
        y_ready, y_copied, y_added = sem("y_ready"), sem("y_copied"), sem("y_added")
        stored = [sem(f"stored{r}") for r in range(2)]
        gathered = [[sem(f"gathered{r}{a}") for a in range(HALVES)] for r in range(2)]
        scattered = sem("scattered")
        act_step, dve_step, pool_step = sem("act_step"), sem("dve_step"), sem("pool_step")

        block = ctx.enter_context(nc.Block())

        def tile(b, j):
            return NT * (b % 2) + j

        def rows_of(m):
            return P if m < MI - 1 else LAST

        def load_expert(sp, w1, w3, w2, free, count):
            for k, (dst, src, loaded) in enumerate(((w1_raw, w1, w1_loaded), (w3_raw, w3, w3_loaded))):
                if free is not None:
                    sp.wait_ge(free, count + k + 1)
                sp.dma_start(dst[:, :, :], src).then_inc(loaded, 16)
            if free is not None:
                sp.wait_ge(free, count + 3)
            sp.dma_start(w2_raw[:, 0:MI - 1, :],
                         w2[0:(MI - 1) * P, :].rearrange("(c p) d -> p c d", p=P)).then_inc(w2_loaded, 16)
            sp.dma_start(w2_raw[0:LAST, MI - 1, :], w2[(MI - 1) * P:I, :]).then_inc(w2_loaded, 16)

        def weight_parts(s):
            return ((w1_raw, w1_hi[s], w1_lo[s]), (w3_raw, w3_hi[s], w3_lo[s]), (w2_raw, w2_hi[s], w2_lo[s]))

        @block.sync
        def _(sp):
            sp.dma_start(ctx_sb[:, 0, :], ctxT[0]).then_inc(ctx_loaded[0], 16)
            sp.dma_start(wq_sb[:, :], WqT).then_inc(wq_loaded, 16)
            sp.dma_start(wk_sb[:, :], WkT).then_inc(wk_loaded, 16)
            sp.dma_start(gamma_c[:, 0:1], gamma_raw.partition_broadcast(P)).then_inc(small_loaded, 16)
            sp.dma_start(bias_b[:, :], gate_b.partition_broadcast(P)).then_inc(small_loaded, 16)
            sp.dma_start(gate_sb[:, :, :], gateT.rearrange("(c p) e -> p c e", p=P)).then_inc(small_loaded, 16)
            def load_batch(b):
                if b:
                    sp.dma_start(ctx_sb[:, b % 2, :], ctxT[b]).then_inc(ctx_loaded[b], 16)
                sp.dma_start(x_sb[:, tile(b, 0):tile(b, 0) + NT, :],
                             x[b].rearrange("(j p) d -> p j d", p=P)).then_inc(x_loaded[b], 16)

            load_batch(0)
            load_expert(sp, Ws1T, Ws3T, Ws2T, None, 0)
            load_batch(1)
            load_expert(sp, W1T[0], W3T[0], W2T[0], shared_split, 0)
            for b in range(B):
                sp.wait_ge(xn_ready, NT * (b + 1))
                sp.dma_start(xn_rows[N * b:N * b + N, :].rearrange("(j p) d -> p j d", p=P),
                             xn[:, :, :]).then_inc(xn_stored, 16)
                if b == B - 1:
                    load_expert(sp, W1T[1], W3T[1], W2T[1], w_split, 0)
                for n in (2 * b, 2 * b + 1):
                    sp.wait_ge(y_added, HALVES * (n + 1))
                    sp.dma_start(out_rows[CAP * n:CAP * n + CAP, :].rearrange("(a p) d -> p a d", p=P),
                                 y_sb[n % 2][:, :, :]).then_inc(stored[n % 2], 16)
                if b + 2 < B:
                    load_batch(b + 2)

            with sp.Fori(2, E) as e:
                load_expert(sp, W1T[e], W3T[e], W2T[e], w_split, 3 * e - 3)
            sp.wait_ge(scattered, 16 * HALVES * E)
            sp.wait_ge(xn_stored, 16 * B)
            for r in range(2):
                sp.wait_ge(stored[r], 16 * (SHARED // 2))

        @block.tensor
        def _(pe):
            def take(name):
                which, k = turns[name]
                if k:
                    pe.wait_ge(drained[which], k)
                return bank[which], filled[which]

            def attention(b):
                pe.wait_ge(ctx_loaded[b], 16)
                if b == 0:
                    pe.wait_ge(wq_loaded, 16)
                dst, done = take(("q", b))
                nc.tensor.matmul(dst[:, :], wq_sb[:, :], ctx_sb[:, b % 2, :], start=True, stop=True).then_inc(done, 1)
                if b == 0:
                    pe.wait_ge(wk_loaded, 16)
                dst, done = take(("k", b))
                nc.tensor.matmul(dst[:, :], wk_sb[:, :], ctx_sb[:, b % 2, :], start=True, stop=True).then_inc(done, 1)
                pe.wait_ge(qk_ready, 2 * (b + 1))
                for j in range(NT):
                    dst, done = take(("sim", b, j))
                    nc.tensor.matmul(dst[:, :], q_sb[:, j * P:(j + 1) * P], k_sb[:, :],
                                     start=True, stop=True).then_inc(done, 1)

            def turn_adjacency(b):
                pe.wait_ge(adj_ready, NT * (b + 1))
                for i in range(NT):
                    dst, done = take(("adjT", b, i))
                    for j in range(NT):
                        last = nc.tensor.transpose(dst[:, j * P:(j + 1) * P], adj[:, j, i * P:(i + 1) * P], ident[:, :])
                    last.then_inc(done, 1)

            def turn_rows(dst, src):
                for c in range(DK):
                    last = nc.tensor.transpose(dst[:, c * P:(c + 1) * P], src[:, c * P:(c + 1) * P], ident[:, :])
                return last

            def batch_rows(b):
                for j in range(NT):
                    pe.wait_ge(xn_ready, NT * b + j + 1)
                    dst, done = take(("xT", b, j))
                    turn_rows(dst, xn[:, j, :]).then_inc(done, 1)

            def gate(b):
                if b == 0:
                    pe.wait_ge(small_loaded, 48)
                dst, done = take(("gate", b))
                for j in range(NT):
                    pe.wait_ge(xT_ready, NT * b + j + 1)
                    for part in (xT_hi, xT_lo):
                        for c in range(DK):
                            rows = part[j // 2][:, c, (j % 2) * P:(j % 2 + 1) * P].bitcast(F32)
                            last = nc.tensor.matmul(dst[:, j * E:(j + 1) * E], rows, gate_sb[:, c, :],
                                                    start=(part is xT_hi and c == 0),
                                                    stop=(part is xT_lo and c == DK - 1))
                last.then_inc(done, 1)

            def places(b):
                pe.wait_ge(mask_ready, b + 1)
                dst, done = take(("place", b))
                nc.tensor.matmul(dst[:, 0:NT * E], upper[:, :], mask[:, :, :], start=True, stop=False)
                nc.tensor.matmul(dst[:, 0:NT * E], ones[:, :], before[:, 0:NT, :],
                                 start=False, stop=True).then_inc(done, 1)

            def slot_table(b):
                pe.wait_ge(hot_ready, b + 1)
                dst, done = take(("table", b))
                if b == 0:
                    for a in range(HALVES):
                        for e in range(E):
                            for h in range(HALVES):
                                at = (3 + a) * COLS + HALVES * e + h
                                nc.tensor.matmul(dst[:, at:at + 1], spare_hot[:, a, e, h * P:(h + 1) * P],
                                                 token_id16[:, a:a + 1], start=True, stop=True)
                for k in range(2):
                    for j in range(NT):
                        last = nc.tensor.matmul(dst[:, 0:3 * COLS], row_hot[:, k, j, :], col_hot[:, :, k, j, :],
                                                start=(k == j == 0), stop=(k == 1 and j == NT - 1))
                last.then_inc(done, 1)

            def three(dst, w, v, first, last):
                nc.tensor.matmul(dst, w[0], v[0], start=first, stop=False)
                nc.tensor.matmul(dst, w[0], v[1], start=False, stop=False)
                return nc.tensor.matmul(dst, w[1], v[0], start=False, stop=last)

            def gate_up(n, r, s):
                pe.wait_ge(xT_ready, HALVES * n + HALVES)
                for m in range(MI):
                    rows = slice(m * P, m * P + rows_of(m))
                    for hi, lo, at in ((w1_hi[s], w1_lo[s], 0), (w3_hi[s], w3_lo[s], CAP)):
                        for c in range(DK):
                            last = three(gu_bank[m][0:rows_of(m), at:at + CAP], (hi[:, c, rows], lo[:, c, rows]),
                                         (xT_hi[r][:, c, :], xT_lo[r][:, c, :]), c == 0, c == DK - 1)
                    last.then_inc(gu_ready, 1)

            def down(n, s):
                for m in range(MI):
                    pe.wait_ge(h_split, MI * n + m + 1)
                    rows = slice(0, rows_of(m))
                    for a in range(HALVES):
                        if m == 0:
                            if not isinstance(n, int) or n > 0:
                                pe.wait_ge(y_copied, HALVES * n - HALVES + a + 1)
                        tokens = slice(a * P, a * P + P)
                        last = three(y_bank[a][:, :], (hidden_hi[rows, m, tokens], hidden_lo[rows, m, tokens]),
                                     (w2_hi[s][rows, m, :], w2_lo[s][rows, m, :]), m == 0, m == MI - 1)
                        if m == MI - 1:
                            last.then_inc(y_ready, 1)

            def expert_rows(n, r, count):
                for a in range(HALVES):
                    pe.wait_ge(gathered[r][a], 16 * count)
                    pe.wait_ge(drained[f"t{a}"], fills[f"t{a}"] + (n - SHARED))
                    turn_rows(bank[f"t{a}"], x_slots[r][:, a, :]).then_inc(filled[f"t{a}"], 1)

            def expert(i, r, more):
                n = SHARED + 2 * i + r
                e = 2 * i + r
                pe.wait_ge(w_split, 3 * e + 2)
                gate_up(n, r, r)
                if more:
                    expert_rows(n + 1, 1 - r, i + 1 + r)
                pe.wait_ge(w_split, 3 * e + 3)
                down(n, r)

            pe.wait_ge(consts_ready, 1)
            attention(0)
            for b in range(B):
                turn_adjacency(b)
                if b + 1 < B:
                    attention(b + 1)
                batch_rows(b)
                gate(b)
                if b == 0:
                    pe.wait_ge(shared_split, 2)
                gate_up(2 * b, 0, 1)
                if b == B - 1:
                    places(b)
                if b == 0:
                    pe.wait_ge(shared_split, 3)
                down(2 * b, 1)
                if b < B - 1:
                    places(b)
                else:
                    slot_table(b)
                gate_up(2 * b + 1, 1, 1)
                if b == B - 1:
                    expert_rows(SHARED, 0, 1)
                down(2 * b + 1, 1)
                if b < B - 1:
                    slot_table(b)
            with pe.Fori(0, E // 2 - 1) as i:
                expert(i, 0, True)
                expert(i, 1, True)
            expert(E // 2 - 1, 0, True)
            expert(E // 2 - 1, 1, False)

        @block.scalar
        def _(act):
            steps = Count()

            def chained(ins):
                ins.then_inc(act_step, 1)
                act.wait_ge(act_step, steps.up())

            def given(name):
                which, k = turns[name]
                act.wait_ge(filled[which], k + 1)
                return bank[which], drained[which]

            def attention(b):
                for name, dst, scale in (("q", q_sb, SIM_SCALE), ("k", k_sb, 1.0)):
                    src, free = given((name, b))
                    nc.scalar.activation(dst[:, :], src[:, :], ACT.Copy, scale=scale).then_inc(qk_ready, 1)
                    free_after(free)
                if b:
                    act.wait_ge(adj_added, NT * b)
                for j in range(NT):
                    src, free = given(("sim", b, j))
                    nc.scalar.activation(sim[:, j, :], src[:, :], ACT.Copy).then_inc(sim_ready, 1)
                    nc.scalar.activation(adj[:, j, :], src[:, :], ACT.Tanh, scale=0.5).then_inc(tanh_ready, 1)
                    free_after(free)

            def free_after(free):
                act.drain().then_inc(free, 1)

            def silu(n, m):
                rows = rows_of(m)
                nc.scalar.activation(silu_g[0:rows, m, :], gu_bank[m][0:rows, 0:CAP],
                                     ACT.Silu).then_inc(silu_ready, 1)

            def hidden_values(n, m):
                act.wait_ge(gu_ready, MI * n + m + 1)
                if n:
                    act.wait_ge(h_ready, MI * (n - 1) + m + 1)
                silu(n, m)
                rows = rows_of(m)
                nc.scalar.activation(up_u[0:rows, m, :], gu_bank[m][0:rows, CAP:2 * CAP], ACT.Copy).then_inc(u_ready, 1)

            def hidden_high(n, m):
                act.wait_ge(h_ready, MI * n + m + 1)
                rows = rows_of(m)
                nc.scalar.activation(hidden_hi[0:rows, m, :], hidden[0:rows, m, :], ACT.Copy).then_inc(h_hi_ready, 1)

            def weight_high(k, s, count, ready):
                raw, hi, _ = weight_parts(s)[k]
                act.wait_ge((w1_loaded, w3_loaded, w2_loaded)[k], (32 if k == 2 else 16) * count)
                nc.scalar.activation(hi[:, :, :], raw[:, :, :], ACT.Copy).then_inc(ready, 1)

            def result(n):
                for a in range(HALVES):
                    act.wait_ge(y_ready, HALVES * n + a + 1)
                    if n >= 2:
                        act.wait_ge(stored[n % 2], 16 * (n // 2))
                    nc.scalar.activation(y_sb[n % 2][:, a, :], y_bank[a][:, :], ACT.Copy).then_inc(y_copied, 1)

            def row_sums(b):
                act.wait_ge(x_loaded[b], 16)
                for j in range(NT):
                    last = nc.scalar.activation(signs[:, j, :], x_sb[:, tile(b, j), :], ACT.Copy, scale=-1.0 / D,
                                                accum_out=x_moment[:, 0, j:j + 1])
                chained(last)
                for j in range(NT):
                    last = nc.scalar.activation(signs[:, j, :], x_sb[:, tile(b, j), :], ACT.Square,
                                                bias=x_moment[:, 0, j:j + 1], accum_out=x_moment[:, 1, j:j + 1])
                chained(last)
                act.sem_inc(x_stats, 1)

            def count(b, k):
                act.wait_ge(probe_ready, SEARCH_STEPS * b + k + 1)
                for j in range(BY_DVE, NT):
                    last = nc.scalar.activation(signs[:, j, :], sim[:, j, :], ACT.Sign, scale=-1.0,
                                                bias=probe[:, 0, j:j + 1], accum_out=probe[:, 1, j:j + 1])
                chained(last)
                act.sem_inc(signs_ready, 1)

            act.wait_ge(small_loaded, 48)
            chained(nc.scalar.activation(gamma_c[:, 1:2], gamma_c[:, 0:1], ACT.Tanh, scale=0.5))
            nc.scalar.activation(gamma_c[:, 2:3], gamma_c[:, 1:2], ACT.Copy, scale=-0.5, bias=0.5)
            nc.scalar.activation(gamma_c[:, 3:4], gamma_c[:, 1:2], ACT.Copy, scale=0.125,
                                 bias=0.125).then_inc(gamma_ready, 1)
            attention(0)
            row_sums(0)
            act.wait_ge(pads_ready, 1)
            for k in range(SEARCH_STEPS):
                count(0, k)
                if k < 3:
                    weight_high(k, 1, 1, shared_hi_ready)
            for b in range(B):
                more = b + 1 < B
                if not more:
                    for k in range(3):
                        weight_high(k, 0, 2, w_hi_ready)
                if more:
                    attention(b + 1)
                for j in range(NT):
                    src, free = given(("xT", b, j))
                    dst = xT_hi[j // 2][:, :, (j % 2) * P:(j % 2 + 1) * P]
                    if b:
                        act.wait_ge(gu_ready, MI * (2 * b - 2 + j // 2) + MI)
                    nc.scalar.activation(dst, src[:, :].rearrange("p (c t) -> p c t", c=DK),
                                         ACT.Copy).then_inc(xT_hi_ready, 1)
                src, free = given(("gate", b))
                if b:
                    act.wait_ge(mask_ready, b)
                chained(nc.scalar.activation(logit[:, :, :], src[:, 0:NT * E].rearrange("p (j e) -> p j e", j=NT),
                                             ACT.Copy))
                act.sem_inc(free, 1)
                act.sem_inc(logit_ready, 1)
                if more:
                    count(b + 1, 0)
                hidden_values(2 * b, 0)
                if more:
                    count(b + 1, 1)
                hidden_values(2 * b, 1)
                hidden_high(2 * b, 0)
                if more:
                    count(b + 1, 2)
                hidden_values(2 * b, 2)
                hidden_high(2 * b, 1)
                chained(nc.scalar.activation(soft[:, :, :], logit[:, :, :], ACT.Abs))
                chained(nc.scalar.activation(soft[:, :, :], soft[:, :, :], ACT.Exp, scale=-1.0))
                nc.scalar.activation(soft[:, :, :], soft[:, :, :], ACT.Ln, bias=1.0).then_inc(soft_ready, 1)
                hidden_high(2 * b, 2)
                if more:
                    count(b + 1, 3)
                act.wait_ge(score_ready, b + 1)
                chained(nc.scalar.activation(rough[:, :, :], score[:, :, :], ACT.Ln))
                nc.scalar.activation(rough[:, :, :], rough[:, :, :], ACT.Exp, scale=0.5).then_inc(rough_ready, 1)
                if more:
                    count(b + 1, 4)
                result(2 * b)
                if more:
                    row_sums(b + 1)
                for m in range(MI):
                    hidden_values(2 * b + 1, m)
                    if m:
                        hidden_high(2 * b + 1, m - 1)
                hidden_high(2 * b + 1, MI - 1)
                result(2 * b + 1)

            def rows_high(n, r):
                for a in range(HALVES):
                    act.wait_ge(filled[f"t{a}"], fills[f"t{a}"] + (n - SHARED) + 1)
                    nc.scalar.activation(xT_hi[r][:, :, a * P:(a + 1) * P],
                                         bank[f"t{a}"][:, :].rearrange("p (c t) -> p c t", c=DK),
                                         ACT.Copy).then_inc(xT_hi_ready, 1)

            def expert(i, r, more=True):
                n = SHARED + 2 * i + r
                e = 2 * i + r
                if more:
                    weight_high(0, 1 - r, e + 3, w_hi_ready)
                act.wait_ge(gu_ready, MI * n + 1)
                silu(n, 0)
                if more:
                    weight_high(1, 1 - r, e + 3, w_hi_ready)
                hidden_high(n, 0)
                act.wait_ge(gu_ready, MI * n + 2)
                silu(n, 1)
                if more:
                    weight_high(2, 1 - r, e + 3, w_hi_ready)
                hidden_high(n, 1)
                act.wait_ge(gu_ready, MI * n + 3)
                silu(n, 2)
                hidden_high(n, 2)
                if more:
                    rows_high(n + 1, 1 - r)
                if isinstance(i, int) and i == 0:
                    act.wait_ge(stored[r], 16 * (SHARED // 2))
                    act.wait_ge(table_ready, 1)
                else:
                    act.wait_ge(scattered, 16 * HALVES * (2 * i + r - 1))
                for a in range(HALVES):
                    act.wait_ge(y_ready, HALVES * n + a + 1)
                    nc.scalar.activation(y_sb[r][:, a, :], y_bank[a][:, :], ACT.Copy,
                                         scale=table[:, 1, bass.ds(HALVES * (2 * i + r) + a, 1)]).then_inc(y_copied, 1)

            rows_high(SHARED, 0)
            expert(0, 0)
            expert(0, 1)
            with act.Fori(1, E // 2 - 1) as i:
                expert(i, 0)
                expert(i, 1)
            expert(E // 2 - 1, 0)
            expert(E // 2 - 1, 1, False)

        @block.vector
        def _(dve):
            steps = Count()

            def mark(ins):
                ins.then_inc(dve_step, 1)
                return steps.up()

            def after(n):
                dve.wait_ge(dve_step, n)

            def chained(ins):
                after(mark(ins))

            def given(name):
                which, k = turns[name]
                dve.wait_ge(filled[which], k + 1)
                return bank[which], drained[which]

            def stats(rows, mv, done):
                for j in range(NT):
                    last = nc.vector.bn_stats(bn[:, j, :], rows(j))
                chained(last)
                for j in range(NT):
                    last = nc.vector.bn_aggr(mv[:, j, :], bn[:, j, :])
                chained(last)
                dve.sem_inc(done, 1)

            def prepare(b):
                dve.wait_ge(sim_ready, NT * (b + 1))
                stats(lambda j: sim[:, j, 0:SAMPLE], mv_s, sim_stats)

            def search(b):
                dve.wait_ge(std_ready, b + 1)
                for dst, z in ((probe[:, 0, :], Z_START), (bracket[:, 0, 0, :], Z_LOW), (bracket[:, 1, 0, :], Z_HIGH)):
                    nc.vector.scalar_tensor_tensor(out=dst, in0=std_s[:, :], scalar=z, in1=mv_s[:, :, 0],
                                                   op0=ALU.mult, op1=ALU.add)
                nc.vector.memset(bracket[:, 0, 1, :], COUNT_LOW)
                chained(nc.vector.memset(bracket[:, 1, 1, :], COUNT_HIGH))
                dve.sem_inc(probe_ready, 1)
                for k in range(SEARCH_STEPS):
                    for j in range(BY_DVE):
                        last = nc.vector.tensor_scalar(above[:, j, :], sim[:, j, :], probe[:, 0, j:j + 1], None,
                                                       ALU.is_ge, ALU.add, accum_out=probe[:, 1, j:j + 1])
                    counted = mark(last)
                    dve.wait_ge(signs_ready, SEARCH_STEPS * b + k + 1)
                    signed = probe[:, 1, BY_DVE:NT]
                    chained(nc.vector.tensor_scalar(signed, signed, -0.5, N / 2.0, ALU.mult, ALU.add))
                    after(counted)
                    nc.vector.tensor_scalar(is_low[:, :], probe[:, 1, :], float(KTH), None, ALU.is_ge)
                    chained(nc.vector.tensor_scalar(is_high[:, :], probe[:, 1, :], float(KTH), None, ALU.is_lt))
                    for side, m in ((0, is_low), (1, is_high)):
                        last = nc.vector.copy_predicated(bracket[:, side, :, :],
                                                         m[:, :].unsqueeze(1).to_broadcast([P, 2, NT]), probe[:, :, :])
                    chained(last)
                    if k == SEARCH_STEPS - 1:
                        break
                    low, high = bracket[:, 0], bracket[:, 1]
                    spread = mark(nc.vector.tensor_tensor(step_a[:, :], low[:, 1, :], high[:, 1, :], ALU.subtract))
                    width = mark(nc.vector.tensor_tensor(step_c[:, :], high[:, 0, :], low[:, 0, :], ALU.subtract))
                    after(spread)
                    chained(nc.vector.reciprocal(step_b[:, :], step_a[:, :]))
                    chained(nc.vector.scalar_tensor_tensor(out=step_b[:, :], in0=low[:, 1, :], scalar=COUNT_AIM,
                                                           in1=step_b[:, :], op0=ALU.subtract, op1=ALU.mult))
                    after(width)
                    chained(nc.vector.scalar_tensor_tensor(out=step_b[:, :], in0=step_b[:, :], scalar=1.0,
                                                           in1=step_c[:, :], op0=ALU.min, op1=ALU.mult))
                    chained(nc.vector.tensor_tensor(probe[:, 0, :], step_b[:, :], low[:, 0, :], ALU.add))
                    dve.sem_inc(probe_ready, 1)

            def threshold(b):
                high_t = bracket[:, 1, 0, :]
                for j in range(NT):
                    last = nc.vector.tensor_scalar(above[:, j, :], sim[:, j, :], high_t[:, j:j + 1], None,
                                                   ALU.is_ge, ALU.add, accum_out=exact[:, j:j + 1])
                chained(last)
                needed = mark(nc.vector.tensor_scalar(need[:, :], exact[:, :], -1.0, float(KTH - 1), ALU.mult, ALU.add))

                def lowered(j):
                    return mark(nc.vector.scalar_tensor_tensor(out=below[j % 2][:, :], in0=above[:, j, :], scalar=-BIG,
                                                               in1=sim[:, j, :], op0=ALU.mult, op1=ALU.add))

                def eight(j):
                    return mark(nc.vector.max(top8[:, j, :], below[j % 2][:, :]))

                first = [lowered(0), lowered(1)]
                after(needed)
                nc.vector.tensor_scalar(step_b[:, :], need[:, :], -0.5, None, ALU.is_lt)
                opened = mark(nc.vector.tensor_scalar(step_a[:, :], need[:, :], 7.5, None, ALU.is_ge))
                after(first[0])
                first[0] = eight(0)
                after(opened)
                opened = mark(nc.vector.tensor_tensor(open_rows[:, :], step_a[:, :], step_b[:, :], ALU.add))
                after(first[1])
                first[1] = eight(1)
                after(opened)
                opened = mark(nc.vector.tensor_reduce(step_a[:, 0:1], open_rows[:, :], AX_X, ALU.add))
                after(first[0])
                second = [lowered(2)]
                after(opened)
                for q in range(4):
                    opened = mark(nc.vector.tensor_copy(open_q[:, q:q + 1], step_a[32 * q:32 * q + 32, 0:1]))
                after(first[1])
                second.append(lowered(3))
                after(opened)
                opened = mark(nc.vector.transpose(open_t[:, :], open_q[:, :]))
                after(second[0])
                second[0] = eight(2)
                after(opened)
                opened = mark(nc.vector.tensor_reduce(open_q[:, 0:1], open_t[:, :], AX_X, ALU.max))
                after(second[1])
                second[1] = eight(3)
                after(opened)
                picking = mark(nc.vector.tensor_tensor(pick8[:, :, :],
                                                       iota_row[:, 0:8].unsqueeze(1).to_broadcast([P, NT, 8]),
                                                       need[:, :].unsqueeze(2).to_broadcast([P, NT, 8]), ALU.is_equal))
                opened = mark(nc.vector.transpose(open_t[:, :], open_q[:, :]))
                after(second[1])
                after(picking)
                picking = mark(nc.vector.tensor_tensor(pick8[:, :, :], pick8[:, :, :], top8[:, :, :], ALU.mult))
                after(opened)
                opened = mark(nc.vector.tensor_reduce(open_q[0:1, 0:1], open_t[0:1, 0:4], AX_X, ALU.max))
                after(picking)
                picking = mark(nc.vector.tensor_reduce(thr[:, :], pick8[:, :, :], AX_X, ALU.add))
                after(opened)
                opened = mark(nc.vector.tensor_copy(open_i[:, :], open_q[0:1, 0:1]))
                after(picking)
                after(opened)
                rows_open = dve.value_load(open_i[0:1, 0:1], min_val=0, max_val=NT)
                with dve.If(rows_open > 0):
                    rest = below[0]
                    for j in range(NT):
                        nc.vector.tensor_copy(rest[:, :], sim[:, j, :])
                        dve.drain()
                        with dve.Fori(0, (KTH - 1) // 8):
                            nc.vector.max(top8[:, j, :], rest[:, :])
                            dve.drain()
                            nc.vector.match_replace(rest[:, :], top8[:, j, :], rest[:, :], -BIG)
                            dve.drain()
                        nc.vector.max(top8[:, j, :], rest[:, :])
                        dve.drain()
                        nc.vector.tensor_copy(thr[:, j:j + 1], top8[:, j, (KTH - 1) % 8:(KTH - 1) % 8 + 1])
                        dve.drain()

            def adjacency(b):
                dve.wait_ge(sig_ready, b + 1)
                for j in range(NT):
                    nc.vector.scalar_tensor_tensor(out=adj[:, j, :], in0=sim[:, j, :], scalar=thr[:, j:j + 1],
                                                   in1=adj[:, j, :], op0=ALU.is_ge, op1=ALU.mult).then_inc(adj_ready, 1)

            def residual(b):
                for j in range(NT):
                    t = tile(b, j)
                    dve.wait_ge(adj_added, NT * b + j + 1)
                    src, free = given(("adjT", b, j))
                    chained(nc.vector.tensor_tensor(x_sb[:, t, :], x_sb[:, t, :], src[:, :], ALU.add))
                    dve.sem_inc(free, 1)
                stats(lambda j: x_sb[:, tile(b, j), :], mv_y, x1_stats)

            def choose(b):
                dve.wait_ge(rough_ready, b + 1)
                chained(nc.vector.reciprocal(soft[:, :, :], rough[:, :, :]))
                chained(nc.vector.tensor_tensor(soft[:, :, :], soft[:, :, :], score[:, :, :], ALU.mult))
                chained(nc.vector.tensor_tensor(score[:, :, :], soft[:, :, :], rough[:, :, :], ALU.add))
                chained(nc.vector.scalar_tensor_tensor(out=biased[:, :, :], in0=score[:, :, :], scalar=0.5,
                                                       in1=bias_b[:, :].unsqueeze(1).to_broadcast([P, NT, E]),
                                                       op0=ALU.mult, op1=ALU.add))
                for j in range(NT):
                    last = nc.vector.max(best[:, j, :], biased[:, j, :])
                chained(last)
                for j in range(NT):
                    last = nc.vector.max_index(best_i[:, j, :], best[:, j, :], biased[:, j, :])
                chained(last)
                chained(nc.vector.tensor_copy(choice[:, :, :], best_i[:, :, 0:2].rearrange("p j k -> p k j")))
                for k in range(2):
                    last = nc.vector.tensor_tensor(onehot[:, k, :, :],
                                                   iota_row[:, 0:E].unsqueeze(1).to_broadcast([P, NT, E]),
                                                   choice[:, k, :].unsqueeze(2).to_broadcast([P, NT, E]), ALU.is_equal)
                chained(last)
                for k in range(2):
                    nc.vector.tensor_tensor(picked[:, k, :, :], onehot[:, k, :, :], score[:, :, :], ALU.mult)
                chained(nc.vector.tensor_tensor(mask[:, :, :], onehot[:, 0, :, :], onehot[:, 1, :, :], ALU.add))
                if b:
                    chained(nc.vector.tensor_copy(before[:, 0, :], before[:, NT, :]))
                for j in range(NT):
                    chained(nc.vector.tensor_tensor(before[:, j + 1, :], before[:, j, :], mask[:, j, :], ALU.add))
                dve.sem_inc(mask_ready, 1)
                chained(nc.vector.tensor_reduce(weight[:, :, :], picked[:, :, :, :], AX_X, ALU.add))
                chained(nc.vector.tensor_tensor(total[:, :], weight[:, 0, :], weight[:, 1, :], ALU.add))
                chained(nc.vector.reciprocal(total[:, :], total[:, :]))
                for k in range(2):
                    last = nc.vector.tensor_tensor(weight[:, k, :], weight[:, k, :], total[:, :], ALU.mult)
                chained(last)

            def place_tokens(b):
                src, free = given(("place", b))
                chained(nc.vector.tensor_copy(place[:, :, :], src[:, 0:NT * E].rearrange("p (j e) -> p j e", j=NT)))
                dve.sem_inc(free, 1)
                for k in range(2):
                    last = nc.vector.tensor_tensor(picked[:, k, :, :], onehot[:, k, :, :], place[:, :, :], ALU.mult)
                chained(last)
                chained(nc.vector.tensor_reduce(slot[:, :, :], picked[:, :, :, :], AX_X, ALU.add))
                chained(nc.vector.tensor_scalar(upper_half[:, :, :], slot[:, :, :], float(P), None, ALU.is_ge))
                chained(nc.vector.scalar_tensor_tensor(out=slot[:, :, :], in0=upper_half[:, :, :], scalar=-float(P),
                                                       in1=slot[:, :, :], op0=ALU.mult, op1=ALU.add))
                chained(nc.vector.scalar_tensor_tensor(out=column[:, :, :], in0=choice[:, :, :], scalar=float(HALVES),
                                                       in1=upper_half[:, :, :], op0=ALU.mult, op1=ALU.add))
                nc.vector.tensor_tensor(row_hot[:, :, :, :],
                                        iota_row[:, :].unsqueeze(1).unsqueeze(1).to_broadcast([P, 2, NT, P]),
                                        slot[:, :, :].unsqueeze(3).to_broadcast([P, 2, NT, P]), ALU.is_equal)
                each = [P, 2, NT, COLS]
                last = nc.vector.tensor_tensor(col_hot[:, 2], iota_row[:, 0:COLS].unsqueeze(1).unsqueeze(1).to_broadcast(each),
                                               column[:, :, :].unsqueeze(3).to_broadcast(each), ALU.is_equal)
                chained(last)
                tokens = token_id[:, NT * b:NT * b + NT]
                nc.vector.tensor_tensor(col_hot[:, 0], col_hot[:, 2],
                                        tokens.unsqueeze(1).unsqueeze(3).to_broadcast(each), ALU.mult)
                last = nc.vector.tensor_tensor(col_hot[:, 1], col_hot[:, 2],
                                               weight[:, :, :].unsqueeze(3).to_broadcast(each), ALU.mult)
                if b == 0:
                    for a in range(HALVES):
                        chained(nc.vector.tensor_scalar(spare[:, a, :], place[:, a, :], token_id[:, a:a + 1],
                                                        float(CAP - 1), ALU.subtract, ALU.add))
                        chained(nc.vector.scalar_tensor_tensor(out=spare[:, a, :], in0=mask[:, a, :],
                                                               scalar=float(2 * CAP), in1=spare[:, a, :],
                                                               op0=ALU.mult, op1=ALU.add))
                        for e in range(E):
                            last = nc.vector.tensor_scalar(spare_hot[:, a, e, :], iota_slot[:, :],
                                                           spare[:, a, e:e + 1], None, ALU.is_equal)
                chained(last)
                dve.sem_inc(hot_ready, 1)

            def add_table(b):
                src, free = given(("table", b))
                got = src[:, 0:3 * COLS].rearrange("p (v c) -> p v c", v=3)
                if b == 0:
                    nc.vector.tensor_copy(table[:, :, :], got)
                    chained(nc.vector.tensor_copy(spare_tab[:, :], src[:, 3 * COLS:4 * COLS]))
                    chained(nc.vector.tensor_tensor(spare_tab[:, :], spare_tab[:, :], src[:, 4 * COLS:5 * COLS], ALU.add))
                else:
                    chained(nc.vector.tensor_tensor(table[:, :, :], table[:, :, :], got, ALU.add))
                dve.sem_inc(free, 1)

            def rows_low(which, count, dst, free):
                dve.wait_ge(xT_hi_ready, count)
                hi, lo = dst
                nc.vector.tensor_tensor(lo, which[:, :].rearrange("p (c t) -> p c t", c=DK), hi.bitcast(F32),
                                        ALU.subtract).then_inc(xT_ready, 1)
                dve.drain().then_inc(free, 1)

            def batch_rows_low(b):
                for j in range(NT):
                    src, free = given(("xT", b, j))
                    at = slice((j % 2) * P, (j % 2 + 1) * P)
                    rows_low(src, NT * b + j + 1, (xT_hi[j // 2][:, :, at], xT_lo[j // 2][:, :, at]), free)

            def weight_low(k, s, count):
                raw, hi, lo = weight_parts(s)[k]
                dve.wait_ge(w_hi_ready, count)
                nc.vector.tensor_tensor(lo[:, :, :], raw[:, :, :], hi[:, :, :].bitcast(F32),
                                        ALU.subtract).then_inc(w_split, 1)

            nc.vector.memset(before[:, 0, :], 0.0)
            nc.vector.memset(open_q[:, :], 0.0)
            prepare(0)
            for b in range(B):
                search(b)
                if b:
                    choose(b - 1)
                threshold(b)
                if b:
                    place_tokens(b - 1)
                adjacency(b)
                if b:
                    add_table(b - 1)
                residual(b)
                if b + 1 < B:
                    prepare(b + 1)
                else:
                    for k in range(3):
                        weight_low(k, 0, k + 1)
                batch_rows_low(b)
            choose(B - 1)
            place_tokens(B - 1)
            add_table(B - 1)
            chained(nc.vector.tensor_scalar(table[:, 2, :], table[:, 2, :], -1.0, 1.0, ALU.mult, ALU.add))
            chained(nc.vector.tensor_tensor(spare_tab[:, :], spare_tab[:, :], table[:, 2, :], ALU.mult))
            nc.vector.tensor_tensor(slot_token[:, :], spare_tab[:, :], table[:, 0, :], ALU.add).then_inc(table_ready, 1)

            def slot_rows_low(n, r):
                for a in range(HALVES):
                    at = slice(a * P, (a + 1) * P)
                    rows_low(bank[f"t{a}"], HALVES * n + a + 1, (xT_hi[r][:, :, at], xT_lo[r][:, :, at]),
                             drained[f"t{a}"])

            def product(n, m):
                rows = rows_of(m)
                dve.wait_ge(silu_ready, MI * n + m + 1)
                nc.vector.tensor_tensor(hidden[0:rows, m, :], silu_g[0:rows, m, :], gu_bank[m][0:rows, CAP:2 * CAP],
                                        ALU.mult).then_inc(h_ready, 1)

            def hidden_low(n, m):
                rows = rows_of(m)
                dve.wait_ge(h_hi_ready, MI * n + m + 1)
                nc.vector.tensor_tensor(hidden_lo[0:rows, m, :], hidden[0:rows, m, :],
                                        hidden_hi[0:rows, m, :].bitcast(F32), ALU.subtract).then_inc(h_split, 1)

            def expert(i, r, more):
                n = SHARED + 2 * i + r
                e = 2 * i + r
                if more:
                    weight_low(0, 1 - r, 3 * e + 4)
                product(n, 0)
                hidden_low(n, 0)
                if more:
                    weight_low(1, 1 - r, 3 * e + 5)
                product(n, 1)
                hidden_low(n, 1)
                if more:
                    weight_low(2, 1 - r, 3 * e + 6)
                product(n, 2)
                hidden_low(n, 2)
                if more:
                    slot_rows_low(n + 1, 1 - r)

            slot_rows_low(SHARED, 0)
            with dve.Fori(0, E // 2 - 1) as i:
                expert(i, 0, True)
                expert(i, 1, True)
            expert(E // 2 - 1, 0, True)
            expert(E // 2 - 1, 1, False)

        @block.gpsimd
        def _(pool):
            steps = Count()

            def chained(ins):
                ins.then_inc(pool_step, 1)
                pool.wait_ge(pool_step, steps.up())

            chained(nc.gpsimd.memset(ones[:, :], 1.0))
            chained(nc.gpsimd.affine_select(out=ident[:, :], in_=ones[:, :], compare_op=ALU.is_equal, fill=0.0,
                                            base=0, pattern=[[1, P]], channel_multiplier=-1))
            chained(nc.gpsimd.affine_select(out=upper[:, :], in_=ones[:, :], compare_op=ALU.is_gt, fill=0.0,
                                            base=0, pattern=[[1, P]], channel_multiplier=-1))
            nc.gpsimd.memset(half_power[:, :], 0.5)
            nc.gpsimd.memset(neg_half_power[:, :], -0.5)
            nc.gpsimd.iota(iota_row[:, :], pattern=[[1, P]], base=0, channel_multiplier=0,
                           allow_small_or_imprecise_dtypes=True)
            nc.gpsimd.iota(iota_slot[:, :], pattern=[[1, CAP]], base=0, channel_multiplier=0,
                           allow_small_or_imprecise_dtypes=True)
            nc.gpsimd.iota(token_id16[:, :], pattern=[[P, HALVES]], base=0, channel_multiplier=1,
                           allow_small_or_imprecise_dtypes=True)
            chained(nc.gpsimd.iota(token_id[:, :], pattern=[[P, TILES]], base=0, channel_multiplier=1,
                                   allow_small_or_imprecise_dtypes=True))
            pool.sem_inc(consts_ready, 1)
            chained(nc.gpsimd.memset(w2_raw[LAST:P, MI - 1, :], 0.0))
            pool.sem_inc(pads_ready, 1)

            def shared_low():
                for k, (raw, hi, lo) in enumerate(weight_parts(1)):
                    pool.wait_ge(shared_hi_ready, k + 1)
                    nc.gpsimd.tensor_tensor(lo[:, :, :], raw[:, :, :], hi[:, :, :].bitcast(F32),
                                            ALU.subtract).then_inc(shared_split, 1)

            def spread(b):
                pool.wait_ge(sim_stats, b + 1)
                nc.gpsimd.tensor_tensor(std_s[:, :], mv_s[:, :, 1], half_power[:, 0:NT], ALU.pow).then_inc(std_ready, 1)

            def sigmoids(b):
                if b == 0:
                    pool.wait_ge(gamma_ready, 1)
                pool.wait_ge(tanh_ready, NT * (b + 1))
                nc.gpsimd.tensor_scalar(adj[:, :, :], adj[:, :, :], 1.0, gamma_c[:, 3:4],
                                        ALU.add, ALU.mult).then_inc(sig_ready, 1)

            def rstd(var):
                chained(nc.gpsimd.tensor_scalar(ln_a[:, :], var, EPS, 1.0, ALU.add, ALU.mult))
                chained(nc.gpsimd.tensor_tensor(ln_a[:, :], ln_a[:, :], neg_half_power[:, :], ALU.pow))

            def base(b):
                pool.wait_ge(x_stats, b + 1)
                chained(nc.gpsimd.tensor_scalar(x_var[:, :], x_moment[:, 1, :], 1.0 / D, 0.0, ALU.mult, ALU.add))
                rstd(x_var[:, :])
                chained(nc.gpsimd.tensor_scalar(ln_a[:, :], ln_a[:, :], gamma_c[:, 2:3], 1.0, ALU.mult, ALU.mult))
                nc.gpsimd.tensor_tensor(ln_add[:, :], x_moment[:, 0, :], ln_a[:, :], ALU.mult)
                chained(nc.gpsimd.tensor_scalar(ln_mul[:, :], ln_a[:, :], 1.0, 1.0, ALU.mult, ALU.add))
                for j in range(NT):
                    t = tile(b, j)
                    last = nc.gpsimd.tensor_scalar(x_sb[:, t, :], x_sb[:, t, :], ln_mul[:, j:j + 1],
                                                   ln_add[:, j:j + 1], ALU.mult, ALU.add)
                chained(last)

            def add_adjacency(b):
                for j in range(NT):
                    t = tile(b, j)
                    pool.wait_ge(adj_ready, NT * b + j + 1)
                    nc.gpsimd.tensor_tensor(x_sb[:, t, :], x_sb[:, t, :], adj[:, j, :],
                                            ALU.add).then_inc(adj_added, 1)

            def normed(b):
                pool.wait_ge(x1_stats, b + 1)
                if b:
                    pool.wait_ge(xn_stored, 16 * b)
                rstd(mv_y[:, :, 1])
                chained(nc.gpsimd.tensor_tensor(ln_add[:, :], mv_y[:, :, 0], ln_a[:, :], ALU.mult))
                chained(nc.gpsimd.tensor_scalar(ln_add[:, :], ln_add[:, :], -1.0, 0.0, ALU.mult, ALU.add))
                for j in range(NT):
                    nc.gpsimd.tensor_scalar(xn[:, j, :], x_sb[:, tile(b, j), :], ln_a[:, j:j + 1],
                                            ln_add[:, j:j + 1], ALU.mult, ALU.add).then_inc(xn_ready, 1)
                pool.wait_ge(xn_ready, NT * (b + 1))

            def scores(b):
                pool.wait_ge(soft_ready, b + 1)
                if b:
                    pool.wait_ge(mask_ready, b)
                chained(nc.gpsimd.tensor_scalar(score[:, :, :], logit[:, :, :], 0.0, 1e-30, ALU.max, ALU.add))
                chained(nc.gpsimd.tensor_tensor(score[:, :, :], score[:, :, :], soft[:, :, :], ALU.add))
                pool.sem_inc(score_ready, 1)

            def hidden_values(n):
                def low(m):
                    rows = rows_of(m)
                    pool.wait_ge(h_hi_ready, MI * n + m + 1)
                    nc.gpsimd.tensor_tensor(hidden_lo[0:rows, m, :], hidden[0:rows, m, :],
                                            hidden_hi[0:rows, m, :].bitcast(F32), ALU.subtract).then_inc(h_split, 1)

                for m in range(MI):
                    rows = rows_of(m)
                    pool.wait_ge(u_ready, MI * n + m + 1)
                    pool.wait_ge(silu_ready, MI * n + m + 1)
                    nc.gpsimd.tensor_tensor(hidden[0:rows, m, :], silu_g[0:rows, m, :], up_u[0:rows, m, :],
                                            ALU.mult).then_inc(h_ready, 1)
                    if m:
                        low(m - 1)
                low(MI - 1)

            def add_residual(n):
                b, half = n // 2, n % 2
                for a in range(HALVES):
                    pool.wait_ge(y_copied, HALVES * n + a + 1)
                    nc.gpsimd.tensor_tensor(y_sb[half][:, a, :], y_sb[half][:, a, :],
                                            x_sb[:, tile(b, HALVES * half + a), :], ALU.add).then_inc(y_added, 1)

            def gather(e):
                r = e % 2
                for a in range(HALVES):
                    if e >= 2:
                        pool.wait_ge(filled[f"t{a}"], fills[f"t{a}"] + e - 1)
                    at = HALVES * e + a
                    nc.gpsimd.indirect_dma_start(
                        out=x_slots[r][:, a, :], out_offset=None, in_=xn_rows[:, :],
                        in_offset=bass.IndirectOffsetOnAxis(ap=slot_token[:, at:at + 1], axis=0),
                    ).then_inc(gathered[r][a], 16)

            def scatter(e):
                for a in range(HALVES):
                    at = HALVES * e + a
                    pool.wait_ge(y_copied, HALVES * (SHARED + e) + a + 1)
                    if at:
                        pool.wait_ge(scattered, 16 * at)
                    nc.gpsimd.indirect_dma_start(
                        out=out_rows[:, :], out_offset=bass.IndirectOffsetOnAxis(ap=slot_token[:, at:at + 1], axis=0),
                        in_=y_sb[e % 2][:, a, :], in_offset=None, compute_op=ALU.add,
                    ).then_inc(scattered, 16)

            spread(0)
            sigmoids(0)
            base(0)
            shared_low()
            add_adjacency(0)
            for b in range(B):
                normed(b)
                more = b + 1 < B
                if more:
                    spread(b + 1)
                if more:
                    sigmoids(b + 1)
                hidden_values(2 * b)
                scores(b)
                add_residual(2 * b)
                if more:
                    base(b + 1)
                hidden_values(2 * b + 1)
                if not more:
                    pool.wait_ge(table_ready, 1)
                    pool.wait_ge(xn_stored, 16 * B)
                    gather(0)
                    gather(1)
                add_residual(2 * b + 1)
                if more:
                    add_adjacency(b + 1)

            for r in range(2):
                pool.wait_ge(stored[r], 16 * (SHARED // 2))
            for e in range(E):
                if e + 2 < E:
                    gather(e + 2)
                scatter(e)


_OUT = (4, 512, 512)


def kernel(x, ctx_512, L0_xattn_Wq, L0_xattn_Wk, L0_xattn_gamma_raw, L0_ffn_input_ids, L0_ffn_gate_w, L0_ffn_gate_b,
           L0_ffn_W1, L0_ffn_W3, L0_ffn_W2, L0_ffn_Ws1, L0_ffn_Ws3, L0_ffn_Ws2):
    import concourse.bacc as _bacc
    from concourse.bass_utils import run_bass_kernel_spmd as _run

    def by_rows(w):
        w = np.swapaxes(np.asarray(w), -1, -2)
        w = w.reshape(w.shape[:-2] + (w.shape[-2] // P, P, w.shape[-1]))
        return np.swapaxes(w, -3, -2)

    laid = {
        "x": np.asarray(x),
        "ctxT": np.swapaxes(np.asarray(ctx_512), 1, 2),
        "WqT": np.asarray(L0_xattn_Wq).T,
        "WkT": np.asarray(L0_xattn_Wk).T,
        "gamma_raw": np.asarray(L0_xattn_gamma_raw).reshape(1),
        "gateT": np.asarray(L0_ffn_gate_w).T,
        "gate_b": np.asarray(L0_ffn_gate_b),
        "W1T": by_rows(L0_ffn_W1),
        "W3T": by_rows(L0_ffn_W3),
        "W2T": np.swapaxes(np.asarray(L0_ffn_W2), 1, 2),
        "Ws1T": by_rows(L0_ffn_Ws1),
        "Ws3T": by_rows(L0_ffn_Ws3),
        "Ws2T": np.asarray(L0_ffn_Ws2).T,
    }
    nc = _bacc.Bacc("TRN2", target_bir_lowering=False, num_devices=1)
    arrays, args = {}, []
    for name, a in laid.items():
        a = np.ascontiguousarray(a)
        arrays[f"in_{name}"] = a
        args.append(nc.dram_tensor(f"in_{name}", a.shape, mybir.dt.from_np(a.dtype), kind="ExternalInput").ap())
    args.append(nc.dram_tensor("out_0", _OUT, F32, kind="ExternalOutput").ap())
    build(nc, *args)
    r = _run(nc, [arrays], core_ids=[0])
    return r.results[0]["out_0"]
```

```python
from contextlib import ExitStack

import numpy as np
import concourse.bass as bass
from concourse import mybir

ALU = mybir.AluOpType
ACT = mybir.ActivationFunctionType
AX_X = mybir.AxisListType.X
F32 = mybir.dt.float32
F32R = mybir.dt.float32r
BF16 = mybir.dt.bfloat16
I32 = mybir.dt.int32
U32 = mybir.dt.uint32

P = 128
EPS = 1e-5
HEADS = 4
TOP_K_RATIO = 0.3
CAP = 256
SEARCH_STEPS = 4
BIG = 1e30


class Count:

    def __init__(self):
        self.value = 0

    def up(self, n=1):
        self.value += n
        return self.value


def bank_turns(batches):
    order = []

    def attn(b):
        order.extend([("t0", ("q", b)), ("t1", ("k", b))])
        order.extend((f"t{j % 2}", ("sim", b, j)) for j in range(4))

    attn(0)
    attn(1)
    order.extend((f"t{j % 2}", ("adjT", 0, j)) for j in range(4))
    for b in range(batches):
        order.extend((f"t{j % 2}", ("xT", b, j)) for j in range(4))
        if b:
            order.append(("s", ("table", b - 1)))
        order.extend([("s", ("gate", b)), ("s", ("logit", b))])
        if b + 1 < batches:
            order.extend((f"t{j % 2}", ("adjT", b + 1, j)) for j in range(4))
        if b + 2 < batches:
            attn(b + 2)
        if b == batches - 1:
            order.append(("s", ("spare",)))
        order.append(("s", ("place", b)))
    order.append(("s", ("table", batches - 1)))
    seen, turns = {}, {}
    for bank, name in order:
        turns[name] = (bank, seen.get(bank, 0))
        seen[bank] = seen.get(bank, 0) + 1
    return turns, seen


def build(nc, x, ctxT, WqT, WkT, gamma_raw, gateT, gate_b, W1T, W3T, W2T, Ws1T, Ws3T, Ws2T, out):
    B, N, D = x.shape
    DC = ctxT.shape[1]
    E, _, DK, I = W1T.shape
    T = B * N
    NT = N // P
    TILES = T // P
    MI = -(-I // P)
    LAST = I - (MI - 1) * P
    HALVES = CAP // P
    COLS = E * HALVES
    KTH = max(1, int(N * TOP_K_RATIO))
    SHARED = T // CAP
    SIM_SCALE = 1.0 / (float(np.sqrt(np.float32(DC // HEADS))) * HEADS)
    Z_START, Z_LOW, Z_HIGH = 0.53, -0.3, 1.3
    COUNT_LOW, COUNT_HIGH, COUNT_AIM = 0.618 * N, 0.097 * N, KTH - 4.5
    DENSITY = 0.32
    BY_DVE = NT // 2
    SAMPLE = N // 2
    assert DC == P and DK == D // P and T % CAP == 0 and HALVES == 2 and NT == 4 and D == N == 512

    x_rows = x.rearrange("b n d -> (b n) d")
    out_rows = out.rearrange("b n d -> (b n) d")
    xn_rows = nc.dram_tensor("xn_rows", [T, D], F32).ap()
    turns, fills = bank_turns(B)

    with ExitStack() as ctx:
        def sb(name, shape, dt=F32):
            return ctx.enter_context(nc.sbuf_tensor(name, shape, dt))

        def sem(name):
            return ctx.enter_context(nc.semaphore(name))

        bank = {n: ctx.enter_context(nc.psum_tensor(f"bank_{n}", [P, 512], F32)) for n in ("t0", "t1", "s")}
        gu_bank = [ctx.enter_context(nc.psum_tensor(f"gu_bank{m}", [P, 512], F32)) for m in range(MI)]
        y_bank = [ctx.enter_context(nc.psum_tensor(f"y_bank{a}", [P, D], F32)) for a in range(HALVES)]

        ident = sb("ident", [P, P])
        upper = sb("upper", [P, P])
        ones = sb("ones", [P, P])
        iota_row = sb("iota_row", [P, P])
        iota_slot = sb("iota_slot", [P, CAP], BF16)
        token_id = sb("token_id", [P, TILES])
        token_id16 = sb("token_id16", [P, HALVES], BF16)
        half_power = sb("half_power", [P, NT])
        neg_half_power = sb("neg_half_power", [P, NT])
        gamma_c = sb("gamma_c", [P, 4])
        bias_b = sb("bias_b", [P, E])
        x_sb = [sb(f"x_sb{r}", [P, NT, D]) for r in range(2)]
        ctx_sb = sb("ctx_sb", [P, 2, N])
        wq_sb = sb("wq_sb", [P, DC])
        wk_sb = sb("wk_sb", [P, DC])
        gate_sb = sb("gate_sb", [P, DK, E])
        gate_hi = sb("gate_hi", [P, DK, E], F32R)
        gate_lo = sb("gate_lo", [P, DK, E], F32R)
        raw_base = nc.sbuf_base
        w1_raw = sb("w1_raw", [P, DK, I])
        w3_raw = sb("w3_raw", [P, DK, I])
        x_sb.append(nc.alloc_sbuf_tensor_at("x_sb2", [P, NT, D], F32, offset=raw_base))
        x_sb.append(x_sb[0])
        w2_raw = sb("w2_raw", [P, MI, D])
        w1_hi, w1_lo, w3_hi, w3_lo, w2_hi, w2_lo = [], [], [], [], [], []
        for r in range(2):
            for name, shape, parts in (("w1", [P, DK, I], (w1_hi, w1_lo)), ("w3", [P, DK, I], (w3_hi, w3_lo)),
                                       ("w2", [P, MI, D], (w2_hi, w2_lo))):
                for part, kept in zip(("hi", "lo"), parts):
                    kept.append(sb(f"{name}_{part}{r}", shape, F32R))
        q_sb = sb("q_sb", [P, N])
        k_sb = sb("k_sb", [P, N])
        sim = [sb(f"sim{r}", [P, NT, N]) for r in range(2)]
        adj = sb("adj", [P, NT, N])
        above = sb("above", [P, NT, N], BF16)
        signs = sb("signs", [P, 2, N], BF16)
        below = [sb(f"below{r}", [P, N]) for r in range(2)]
        spare_hot = [sim[a][:, :, :].bitcast(BF16).rearrange("p j (q c) -> p (j q) c", c=CAP) for a in range(HALVES)]
        probe = sb("probe", [P, 2, NT])
        bracket = sb("bracket", [P, 2, 2, NT])
        is_low = sb("is_low", [P, NT], I32)
        is_high = sb("is_high", [P, NT], I32)
        step_a = sb("step_a", [P, NT])
        step_b = sb("step_b", [P, NT])
        step_c = sb("step_c", [P, NT])
        slope = sb("slope", [P, NT])
        exact = sb("exact", [P, NT])
        need = sb("need", [P, NT])
        top8 = sb("top8", [P, NT, 8])
        pick8 = sb("pick8", [P, NT, 8])
        value8 = sb("value8", [P, NT, 8])
        thr = sb("thr", [P, NT])
        open_rows = sb("open_rows", [P, NT])
        open_q = sb("open_q", [32, 32])
        open_t = sb("open_t", [32, 32])
        open_i = sb("open_i", [1, 1], I32)
        bn = sb("bn", [P, NT, 6])
        x_moment = sb("x_moment", [P, 2, 2, NT])
        x_var = sb("x_var", [P, NT])
        mv_s = sb("mv_s", [P, NT, 2])
        mv_y = sb("mv_y", [P, NT, 2])
        std_s = sb("std_s", [P, NT])
        ln_a = sb("ln_a", [P, NT])
        ln_mul = sb("ln_mul", [P, NT])
        ln_add = sb("ln_add", [P, NT])
        xn = sb("xn", [P, NT, D])
        xT_hi = [sb(f"xT_hi{r}", [P, DK, CAP], F32R) for r in range(2)]
        xT_lo = [sb(f"xT_lo{r}", [P, DK, CAP], F32R) for r in range(2)]
        logitT = q_sb[0:E, :]
        logit = sb("logit", [P, NT, E])
        soft = sb("soft", [P, NT, E])
        rough = sb("rough", [P, NT, E])
        score = sb("score", [P, NT, E])
        biased = sb("biased", [P, NT, E])
        best = sb("best", [P, NT, 8])
        best_i = sb("best_i", [P, NT, 8], U32)
        choice = sb("choice", [P, 2, NT])
        onehot = sb("onehot", [P, 2, NT, E])
        picked = sb("picked", [P, 2, NT, E])
        weight = sb("weight", [P, 2, NT])
        total = sb("total", [P, NT])
        mask = sb("mask", [P, NT, E])
        before = sb("before", [P, NT + 1, E])
        place = sb("place", [P, NT, E])
        slot = sb("slot", [P, 2, NT])
        upper_half = sb("upper_half", [P, 2, NT])
        column = sb("column", [P, 2, NT])
        spare = sb("spare", [P, HALVES, E])
        row_hot = sb("row_hot", [P, 2, NT, P])
        col_hot = sb("col_hot", [P, 3, 2, NT, COLS])
        table = sb("table", [P, 3, COLS])
        spare_tab = sb("spare_tab", [P, COLS])
        slot_token = sb("slot_token", [P, COLS], I32)
        x_slots = [xn[:, HALVES * r:HALVES * r + HALVES, :] for r in range(2)]
        silu_g = sb("silu_g", [P, MI, CAP])
        up_u = sb("up_u", [P, MI, CAP])
        hidden = sb("hidden", [P, MI, CAP])
        hidden_hi = sb("hidden_hi", [P, MI, CAP], F32R)
        hidden_lo = sb("hidden_lo", [P, MI, CAP], F32R)
        y_sb = [sb(f"y_sb{r}", [P, HALVES, D]) for r in range(2)]

        wq_loaded, wk_loaded, small_loaded = sem("wq_loaded"), sem("wk_loaded"), sem("small_loaded")
        ctx_loaded = [sem(f"ctx_loaded{b}") for b in range(B)]
        x_loaded = [sem(f"x_loaded{b}") for b in range(B)]
        w1_loaded, w3_loaded, w2_loaded = sem("w1_loaded"), sem("w3_loaded"), sem("w2_loaded")
        shared_hi_ready, shared_split = sem("shared_hi_ready"), sem("shared_split")
        w_hi_ready, w_split = sem("w_hi_ready"), sem("w_split")
        consts_ready = sem("consts_ready")
        pads_ready = sem("pads_ready")
        gamma_ready, gate_hi_ready, gate_split = sem("gamma_ready"), sem("gate_hi_ready"), sem("gate_split")
        filled = {n: sem(f"filled_{n}") for n in bank}
        drained = {n: sem(f"drained_{n}") for n in bank}
        qk_ready = sem("qk_ready")
        sim_ready, tanh_ready = sem("sim_ready"), sem("tanh_ready")
        sim_stats, std_ready = sem("sim_stats"), sem("std_ready")
        sig_ready, adj_ready, adj_added = sem("sig_ready"), sem("adj_ready"), sem("adj_added")
        probe_ready, signs_ready = sem("probe_ready"), sem("signs_ready")
        x_stats = sem("x_stats")
        x1_stats, xn_ready, xn_stored = sem("x1_stats"), sem("xn_ready"), sem("xn_stored")
        soft_ready, score_ready, rough_ready = sem("soft_ready"), sem("score_ready"), sem("rough_ready")
        mask_ready, hot_ready, table_ready = sem("mask_ready"), sem("hot_ready"), sem("table_ready")
        spare_hot_ready = sem("spare_hot_ready")
        logitT_ready = sem("logitT_ready")
        xT_hi_ready = sem("xT_hi_ready")
        gu_ready, silu_ready, u_ready = sem("gu_ready"), sem("silu_ready"), sem("u_ready")
        h_ready, h_hi_ready, h_split = sem("h_ready"), sem("h_hi_ready"), sem("h_split")
        y_ready, y_copied, y_added = sem("y_ready"), sem("y_copied"), sem("y_added")
        stored = [sem(f"stored{r}") for r in range(2)]
        gathered = [[sem(f"gathered{r}{a}") for a in range(HALVES)] for r in range(2)]
        scattered = sem("scattered")
        act_step, dve_step, pool_step = sem("act_step"), sem("dve_step"), sem("pool_step")

        block = ctx.enter_context(nc.Block())

        def rows_of(m):
            return P if m < MI - 1 else LAST

        def load_w13(sp, w1, w3, free, count):
            for k, (dst, src, loaded) in enumerate(((w1_raw, w1, w1_loaded), (w3_raw, w3, w3_loaded))):
                if free is not None:
                    sp.wait_ge(free, count + k + 1)
                sp.dma_start(dst[:, :, :], src).then_inc(loaded, 16)

        def load_w2(sp, w2, free, count):
            if free is not None:
                sp.wait_ge(free, count + 3)
            sp.dma_start(w2_raw[:, 0:MI - 1, :],
                         w2[0:(MI - 1) * P, :].rearrange("(c p) d -> p c d", p=P)).then_inc(w2_loaded, 16)
            sp.dma_start(w2_raw[0:LAST, MI - 1, :], w2[(MI - 1) * P:I, :]).then_inc(w2_loaded, 16)

        def weight_parts(s):
            return ((w1_raw, w1_hi[s], w1_lo[s]), (w3_raw, w3_hi[s], w3_lo[s]), (w2_raw, w2_hi[s], w2_lo[s]))

        @block.sync
        def _(sp):
            sp.dma_start(ctx_sb[:, 0, :], ctxT[0]).then_inc(ctx_loaded[0], 16)
            sp.dma_start(wq_sb[:, :], WqT).then_inc(wq_loaded, 16)
            sp.dma_start(wk_sb[:, :], WkT).then_inc(wk_loaded, 16)
            sp.dma_start(gamma_c[:, 0:1], gamma_raw.partition_broadcast(P)).then_inc(small_loaded, 16)
            sp.dma_start(bias_b[:, :], gate_b.partition_broadcast(P)).then_inc(small_loaded, 16)
            sp.dma_start(gate_sb[:, :, :], gateT.rearrange("(c p) e -> p c e", p=P)).then_inc(small_loaded, 16)
            def load_context(b):
                if b >= 2:
                    sp.wait_ge(qk_ready, 2 * (b - 1))
                sp.dma_start(ctx_sb[:, b % 2, :], ctxT[b]).then_inc(ctx_loaded[b], 16)

            def load_batch(b):
                sp.dma_start(x_sb[b][:, :, :],
                             x[b].rearrange("(j p) d -> p j d", p=P)).then_inc(x_loaded[b], 16)

            load_context(1)
            load_batch(0)
            load_w13(sp, Ws1T, Ws3T, None, 0)
            load_w2(sp, Ws2T, None, 0)
            load_batch(1)
            sp.wait_ge(shared_split, 2)
            load_batch(2)
            load_w2(sp, W2T[0], shared_split, 0)
            for b in range(B):
                if b + 2 < B:
                    load_context(b + 2)
                sp.wait_ge(xn_ready, NT * (b + 1))
                sp.dma_start(xn_rows[N * b:N * b + N, :].rearrange("(j p) d -> p j d", p=P),
                             xn[:, :, :]).then_inc(xn_stored, 16)
                if b == B - 1:
                    load_w13(sp, W1T[1], W3T[1], w_split, 0)
                    load_w2(sp, W2T[1], w_split, 0)
                for n in (2 * b, 2 * b + 1):
                    sp.wait_ge(y_added, HALVES * (n + 1))
                    sp.dma_start(out_rows[CAP * n:CAP * n + CAP, :].rearrange("(a p) d -> p a d", p=P),
                                 y_sb[n % 2][:, :, :]).then_inc(stored[n % 2], 16)
                if b == 0:
                    load_batch(3)
                if b == 2:
                    load_w13(sp, W1T[0], W3T[0], None, 0)

            with sp.Fori(2, E) as e:
                load_w13(sp, W1T[e], W3T[e], w_split, 3 * e - 3)
                load_w2(sp, W2T[e], w_split, 3 * e - 3)
            sp.wait_ge(scattered, 16 * HALVES * E)
            sp.wait_ge(xn_stored, 16 * B)
            for r in range(2):
                sp.wait_ge(stored[r], 16 * (SHARED // 2))

        @block.tensor
        def _(pe):
            def take(name):
                which, k = turns[name]
                if k:
                    pe.wait_ge(drained[which], k)
                return bank[which], filled[which]

            def rows_there(n):
                for a in range(HALVES):
                    if isinstance(n, int) and n < SHARED:
                        which, k = turns[("xT", n // 2, HALVES * (n % 2) + a)]
                        pe.wait_ge(drained[which], k + 1)
                    else:
                        pe.wait_ge(drained[f"t{a}"], fills[f"t{a}"] + (n - SHARED) + 1)

            def attention(b):
                pe.wait_ge(ctx_loaded[b], 16)
                if b == 0:
                    pe.wait_ge(wq_loaded, 16)
                dst, done = take(("q", b))
                nc.tensor.matmul(dst[:, :], wq_sb[:, :], ctx_sb[:, b % 2, :], start=True, stop=True).then_inc(done, 1)
                if b == 0:
                    pe.wait_ge(wk_loaded, 16)
                dst, done = take(("k", b))
                nc.tensor.matmul(dst[:, :], wk_sb[:, :], ctx_sb[:, b % 2, :], start=True, stop=True).then_inc(done, 1)
                pe.wait_ge(qk_ready, 2 * (b + 1))
                for j in range(NT):
                    dst, done = take(("sim", b, j))
                    nc.tensor.matmul(dst[:, :], q_sb[:, j * P:(j + 1) * P], k_sb[:, :],
                                     start=True, stop=True).then_inc(done, 1)

            def turn_adjacency(b):
                pe.wait_ge(adj_ready, NT * (b + 1))
                for i in range(NT):
                    dst, done = take(("adjT", b, i))
                    for j in range(NT):
                        last = nc.tensor.transpose(dst[:, j * P:(j + 1) * P], adj[:, j, i * P:(i + 1) * P], ident[:, :])
                    last.then_inc(done, 1)

            def turn_rows(dst, src):
                for c in range(DK):
                    last = nc.tensor.transpose(dst[:, c * P:(c + 1) * P], src[:, c * P:(c + 1) * P], ident[:, :])
                return last

            def batch_rows(b):
                for j in range(NT):
                    pe.wait_ge(xn_ready, NT * b + j + 1)
                    dst, done = take(("xT", b, j))
                    turn_rows(dst, xn[:, j, :]).then_inc(done, 1)

            def three(dst, w, v, first, last):
                nc.tensor.matmul(dst, w[0], v[0], start=first, stop=False)
                nc.tensor.matmul(dst, w[0], v[1], start=False, stop=False)
                return nc.tensor.matmul(dst, w[1], v[0], start=False, stop=last)

            def gate(b):
                if b == 0:
                    pe.wait_ge(gate_split, 1)
                dst, done = take(("gate", b))
                for r in range(HALVES):
                    rows_there(2 * b + r)
                    for c in range(DK):
                        last = three(dst[0:E, r * CAP:(r + 1) * CAP], (gate_hi[:, c, :], gate_lo[:, c, :]),
                                     (xT_hi[r][:, c, :], xT_lo[r][:, c, :]), c == 0, c == DK - 1)
                last.then_inc(done, 1)

            def turn_logits(b):
                pe.wait_ge(logitT_ready, b + 1)
                dst, done = take(("logit", b))
                for j in range(NT):
                    last = nc.tensor.transpose(dst[:, j * E:(j + 1) * E], logitT[:, j * P:(j + 1) * P],
                                               ident[0:E, 0:E])
                last.then_inc(done, 1)

            def places(b):
                pe.wait_ge(mask_ready, b + 1)
                dst, done = take(("place", b))
                nc.tensor.matmul(dst[:, 0:NT * E], upper[:, :], mask[:, :, :], start=True, stop=False)
                nc.tensor.matmul(dst[:, 0:NT * E], ones[:, :], before[:, 0:NT, :],
                                 start=False, stop=True).then_inc(done, 1)

            def spare_tokens():
                pe.wait_ge(spare_hot_ready, HALVES)
                dst, done = take(("spare",))
                for a in range(HALVES):
                    for e in range(E):
                        for h in range(HALVES):
                            at = COLS * a + HALVES * e + h
                            last = nc.tensor.matmul(dst[:, at:at + 1], spare_hot[a][:, e, h * P:(h + 1) * P],
                                                    token_id16[:, a:a + 1], start=True, stop=True)
                last.then_inc(done, 1)

            def slot_table(b):
                pe.wait_ge(hot_ready, b + 1)
                dst, done = take(("table", b))
                for k in range(2):
                    for j in range(NT):
                        last = nc.tensor.matmul(dst[:, 0:3 * COLS], row_hot[:, k, j, :], col_hot[:, :, k, j, :],
                                                start=(k == j == 0), stop=(k == 1 and j == NT - 1))
                last.then_inc(done, 1)

            def gate_up(n, r, s, chunks=range(MI)):
                rows_there(n)
                for m in chunks:
                    rows = slice(m * P, m * P + rows_of(m))
                    for hi, lo, at in ((w1_hi[s], w1_lo[s], 0), (w3_hi[s], w3_lo[s], CAP)):
                        for c in range(DK):
                            last = three(gu_bank[m][0:rows_of(m), at:at + CAP], (hi[:, c, rows], lo[:, c, rows]),
                                         (xT_hi[r][:, c, :], xT_lo[r][:, c, :]), c == 0, c == DK - 1)
                    last.then_inc(gu_ready, 1)

            def down(n, s):
                for m in range(MI):
                    pe.wait_ge(h_split, MI * n + m + 1)
                    rows = slice(0, rows_of(m))
                    for a in range(HALVES):
                        if m == 0:
                            if not isinstance(n, int) or n > 0:
                                pe.wait_ge(y_copied, HALVES * n - HALVES + a + 1)
                        tokens = slice(a * P, a * P + P)
                        last = three(y_bank[a][:, :], (hidden_hi[rows, m, tokens], hidden_lo[rows, m, tokens]),
                                     (w2_hi[s][rows, m, :], w2_lo[s][rows, m, :]), m == 0, m == MI - 1)
                        if m == MI - 1:
                            last.then_inc(y_ready, 1)

            def expert_rows(n, r, count):
                for a in range(HALVES):
                    pe.wait_ge(gathered[r][a], 16 * count)
                    pe.wait_ge(drained[f"t{a}"], fills[f"t{a}"] + (n - SHARED))
                    turn_rows(bank[f"t{a}"], x_slots[r][:, a, :]).then_inc(filled[f"t{a}"], 1)

            def expert(i, r, more):
                n = SHARED + 2 * i + r
                e = 2 * i + r
                pe.wait_ge(w_split, 3 * e + 2)
                gate_up(n, r, r)
                if more:
                    expert_rows(n + 1, 1 - r, i + 1 + r)
                pe.wait_ge(w_split, 3 * e + 3)
                down(n, r)

            pe.wait_ge(consts_ready, 1)
            attention(0)
            attention(1)
            turn_adjacency(0)
            for b in range(B):
                batch_rows(b)
                if b:
                    slot_table(b - 1)
                gate(b)
                if b == 0:
                    pe.wait_ge(shared_split, 2)
                gate_up(2 * b, 0, 1, range(1))
                turn_logits(b)
                gate_up(2 * b, 0, 1, range(1, MI))
                if b == B - 1:
                    spare_tokens()
                if b == 0:
                    pe.wait_ge(shared_split, 3)
                down(2 * b, 1)
                if b + 1 < B:
                    turn_adjacency(b + 1)
                if b + 2 < B:
                    attention(b + 2)
                if b + 1 < B:
                    gate_up(2 * b + 1, 1, 1)
                    places(b)
                    down(2 * b + 1, 1)
            gate_up(SHARED - 1, 1, 1, range(1))
            places(B - 1)
            gate_up(SHARED - 1, 1, 1, range(1, MI))
            slot_table(B - 1)
            down(SHARED - 1, 1)
            expert_rows(SHARED, 0, 1)
            with pe.Fori(0, E // 2 - 1) as i:
                expert(i, 0, True)
                expert(i, 1, True)
            expert(E // 2 - 1, 0, True)
            expert(E // 2 - 1, 1, False)

        @block.scalar
        def _(act):
            steps = Count()

            def chained(ins):
                ins.then_inc(act_step, 1)
                act.wait_ge(act_step, steps.up())

            def given(name):
                which, k = turns[name]
                act.wait_ge(filled[which], k + 1)
                return bank[which], drained[which]

            def attention(b):
                for name, dst, scale in (("q", q_sb, SIM_SCALE), ("k", k_sb, 1.0)):
                    src, free = given((name, b))
                    nc.scalar.activation(dst[:, :], src[:, :], ACT.Copy, scale=scale).then_inc(qk_ready, 1)
                    free_after(free)
                for j in range(NT):
                    if b >= 2:
                        act.wait_ge(adj_ready, NT * (b - 1))
                    src, free = given(("sim", b, j))
                    nc.scalar.activation(sim[b % 2][:, j, :], src[:, :], ACT.Copy).then_inc(sim_ready, 1)
                    free_after(free)

            def tanhs(b):
                if b:
                    act.wait_ge(adj_added, NT * b)
                act.wait_ge(sim_ready, NT * (b + 1))
                nc.scalar.activation(adj[:, :, :], sim[b % 2][:, :, :], ACT.Tanh, scale=0.5).then_inc(tanh_ready, 1)

            def free_after(free):
                act.drain().then_inc(free, 1)

            def silu(n, m):
                rows = rows_of(m)
                nc.scalar.activation(silu_g[0:rows, m, :], gu_bank[m][0:rows, 0:CAP],
                                     ACT.Silu).then_inc(silu_ready, 1)

            def hidden_values(n, m):
                act.wait_ge(gu_ready, MI * n + m + 1)
                if n:
                    act.wait_ge(h_ready, MI * (n - 1) + m + 1)
                silu(n, m)
                rows = rows_of(m)
                nc.scalar.activation(up_u[0:rows, m, :], gu_bank[m][0:rows, CAP:2 * CAP], ACT.Copy).then_inc(u_ready, 1)

            def hidden_high(n, m):
                act.wait_ge(h_ready, MI * n + m + 1)
                rows = rows_of(m)
                nc.scalar.activation(hidden_hi[0:rows, m, :], hidden[0:rows, m, :], ACT.Copy).then_inc(h_hi_ready, 1)

            def weight_high(k, s, count, ready):
                raw, hi, _ = weight_parts(s)[k]
                act.wait_ge((w1_loaded, w3_loaded, w2_loaded)[k], (32 if k == 2 else 16) * count)
                nc.scalar.activation(hi[:, :, :], raw[:, :, :], ACT.Copy).then_inc(ready, 1)

            def result(n):
                for a in range(HALVES):
                    act.wait_ge(y_ready, HALVES * n + a + 1)
                    if n >= 2:
                        act.wait_ge(stored[n % 2], 16 * (n // 2))
                    nc.scalar.activation(y_sb[n % 2][:, a, :], y_bank[a][:, :], ACT.Copy).then_inc(y_copied, 1)

            def row_sums(b, k):
                if k == 0:
                    act.wait_ge(x_loaded[b], 16)
                for j in range(NT):
                    f, shift = ((ACT.Copy, {"scale": -1.0 / D}), (ACT.Square, {"bias": x_moment[:, b % 2, 0, j:j + 1]}))[k]
                    last = nc.scalar.activation(signs[:, j % 2, :], x_sb[b][:, j, :], f,
                                                accum_out=x_moment[:, b % 2, k, j:j + 1], **shift)
                    if j % 2:
                        chained(last)
                if k == 1:
                    act.sem_inc(x_stats, 1)

            def count(b, k):
                act.wait_ge(probe_ready, SEARCH_STEPS * b + k + 1)
                for j in range(BY_DVE, NT):
                    last = nc.scalar.activation(signs[:, j % 2, :], sim[b % 2][:, j, :], ACT.Sign, scale=-1.0,
                                                bias=probe[:, 0, j:j + 1], accum_out=probe[:, 1, j:j + 1])
                chained(last)
                act.sem_inc(signs_ready, 1)

            act.wait_ge(small_loaded, 48)
            chained(nc.scalar.activation(gamma_c[:, 1:2], gamma_c[:, 0:1], ACT.Tanh, scale=0.5))
            nc.scalar.activation(gamma_c[:, 2:3], gamma_c[:, 1:2], ACT.Copy, scale=-0.5, bias=0.5)
            nc.scalar.activation(gamma_c[:, 3:4], gamma_c[:, 1:2], ACT.Copy, scale=0.125,
                                 bias=0.125).then_inc(gamma_ready, 1)
            nc.scalar.activation(gate_hi[:, :, :], gate_sb[:, :, :], ACT.Copy).then_inc(gate_hi_ready, 1)
            def batch_rows_high(b, tiles):
                for j in tiles:
                    src, _ = given(("xT", b, j))
                    dst = xT_hi[j // 2][:, :, (j % 2) * P:(j % 2 + 1) * P]
                    if b:
                        act.wait_ge(gu_ready, MI * (2 * b - 2 + j // 2) + MI)
                    nc.scalar.activation(dst, src[:, :].rearrange("p (c t) -> p c t", c=DK),
                                         ACT.Copy).then_inc(xT_hi_ready, 1)

            def softplus_part(b):
                chained(nc.scalar.activation(soft[:, :, :], logit[:, :, :], ACT.Abs))
                chained(nc.scalar.activation(soft[:, :, :], soft[:, :, :], ACT.Exp, scale=-1.0))
                nc.scalar.activation(soft[:, :, :], soft[:, :, :], ACT.Ln, bias=1.0).then_inc(soft_ready, 1)

            attention(0)
            count(0, 0)
            count(0, 1)
            count(0, 2)
            count(0, 3)
            tanhs(0)
            row_sums(0, 0)
            row_sums(0, 1)
            attention(1)
            act.wait_ge(pads_ready, 1)
            for k in range(3):
                weight_high(k, 1, 1, shared_hi_ready)
            count(1, 0)
            row_sums(1, 0)
            row_sums(1, 1)
            for b in range(B):
                more = b + 1 < B
                done = 1 if b == 0 else 2
                batch_rows_high(b, (0, 1))
                if more:
                    count(b + 1, done)
                batch_rows_high(b, (2, 3))
                if more:
                    count(b + 1, done + 1)
                src, free = given(("gate", b))
                chained(nc.scalar.activation(logitT[:, :], src[0:E, :], ACT.Copy))
                act.sem_inc(free, 1)
                act.sem_inc(logitT_ready, 1)
                if more:
                    if b == 0:
                        count(b + 1, 3)
                    hidden_values(2 * b, 0)
                src, free = given(("logit", b))
                if b:
                    act.wait_ge(mask_ready, b)
                chained(nc.scalar.activation(logit[:, :, :], src[:, 0:NT * E].rearrange("p (j e) -> p j e", j=NT),
                                             ACT.Copy))
                act.sem_inc(free, 1)
                if not more:
                    softplus_part(b)
                    hidden_values(2 * b, 0)
                hidden_values(2 * b, 1)
                hidden_high(2 * b, 0)
                if more:
                    tanhs(b + 1)
                hidden_values(2 * b, 2)
                hidden_high(2 * b, 1)
                hidden_high(2 * b, 2)
                if more:
                    softplus_part(b)
                act.wait_ge(score_ready, b + 1)
                chained(nc.scalar.activation(rough[:, :, :], score[:, :, :], ACT.Ln))
                nc.scalar.activation(rough[:, :, :], rough[:, :, :], ACT.Exp, scale=0.5).then_inc(rough_ready, 1)
                result(2 * b)
                if b + 2 < B:
                    row_sums(b + 2, 0)
                    row_sums(b + 2, 1)
                    attention(b + 2)
                if not more:
                    for k in range(3):
                        weight_high(k, 0, 2, w_hi_ready)
                for m in range(MI):
                    hidden_values(2 * b + 1, m)
                    if m:
                        hidden_high(2 * b + 1, m - 1)
                    if m == 0 and b + 2 < B:
                        count(b + 2, 0)
                    if m == 1 and b + 2 < B:
                        count(b + 2, 1)
                hidden_high(2 * b + 1, MI - 1)
                result(2 * b + 1)

            def rows_high(n, r):
                for a in range(HALVES):
                    act.wait_ge(filled[f"t{a}"], fills[f"t{a}"] + (n - SHARED) + 1)
                    nc.scalar.activation(xT_hi[r][:, :, a * P:(a + 1) * P],
                                         bank[f"t{a}"][:, :].rearrange("p (c t) -> p c t", c=DK),
                                         ACT.Copy).then_inc(xT_hi_ready, 1)

            def expert(i, r, more=True):
                n = SHARED + 2 * i + r
                e = 2 * i + r
                if more:
                    weight_high(0, 1 - r, e + 3, w_hi_ready)
                act.wait_ge(gu_ready, MI * n + 1)
                silu(n, 0)
                if more:
                    weight_high(1, 1 - r, e + 3, w_hi_ready)
                hidden_high(n, 0)
                act.wait_ge(gu_ready, MI * n + 2)
                silu(n, 1)
                if more:
                    weight_high(2, 1 - r, e + 3, w_hi_ready)
                hidden_high(n, 1)
                act.wait_ge(gu_ready, MI * n + 3)
                silu(n, 2)
                hidden_high(n, 2)
                if more:
                    rows_high(n + 1, 1 - r)
                if isinstance(i, int) and i == 0:
                    act.wait_ge(stored[r], 16 * (SHARED // 2))
                    act.wait_ge(table_ready, 1)
                else:
                    act.wait_ge(scattered, 16 * HALVES * (2 * i + r - 1))
                for a in range(HALVES):
                    act.wait_ge(y_ready, HALVES * n + a + 1)
                    nc.scalar.activation(y_sb[r][:, a, :], y_bank[a][:, :], ACT.Copy,
                                         scale=table[:, 1, bass.ds(HALVES * (2 * i + r) + a, 1)]).then_inc(y_copied, 1)

            rows_high(SHARED, 0)
            expert(0, 0)
            expert(0, 1)
            with act.Fori(1, E // 2 - 1) as i:
                expert(i, 0)
                expert(i, 1)
            expert(E // 2 - 1, 0)
            expert(E // 2 - 1, 1, False)

        @block.vector
        def _(dve):
            steps = Count()

            def mark(ins):
                ins.then_inc(dve_step, 1)
                return steps.up()

            def after(n):
                dve.wait_ge(dve_step, n)

            def chained(ins):
                after(mark(ins))

            def given(name):
                which, k = turns[name]
                dve.wait_ge(filled[which], k + 1)
                return bank[which], drained[which]

            def aggregate(last, mv, done):
                chained(last)
                for j in range(NT):
                    last = nc.vector.bn_aggr(mv[:, j, :], bn[:, j, :])
                chained(last)
                dve.sem_inc(done, 1)

            def prepare(b):
                for j in range(NT):
                    dve.wait_ge(sim_ready, NT * b + j + 1)
                    last = nc.vector.bn_stats(bn[:, j, :], sim[b % 2][:, j, 0:SAMPLE])
                aggregate(last, mv_s, sim_stats)

            def start(b):
                dve.wait_ge(std_ready, b + 1)
                for dst, z in ((probe[:, 0, :], Z_START), (bracket[:, 0, 0, :], Z_LOW), (bracket[:, 1, 0, :], Z_HIGH)):
                    nc.vector.scalar_tensor_tensor(out=dst, in0=std_s[:, :], scalar=z, in1=mv_s[:, :, 0],
                                                   op0=ALU.mult, op1=ALU.add)
                nc.vector.tensor_scalar(slope[:, :], std_s[:, :], -1.0 / (2 * N * DENSITY), None, ALU.mult)
                nc.vector.memset(bracket[:, 0, 1, :], N - 2 * COUNT_LOW)
                chained(nc.vector.memset(bracket[:, 1, 1, :], N - 2 * COUNT_HIGH))
                dve.sem_inc(probe_ready, 1)

            def search(b, k):
                for j in range(BY_DVE):
                    last = nc.vector.tensor_scalar(above[:, j, :], sim[b % 2][:, j, :], probe[:, 0, j:j + 1], None,
                                                   ALU.is_ge, ALU.add, accum_out=probe[:, 1, j:j + 1])
                chained(last)
                mine = probe[:, 1, 0:BY_DVE]
                chained(nc.vector.tensor_scalar(mine, mine, -2.0, float(N), ALU.mult, ALU.add))
                dve.wait_ge(signs_ready, SEARCH_STEPS * b + k + 1)
                if k == 0:
                    nc.vector.scalar_tensor_tensor(out=step_b[:, :], in0=probe[:, 1, :], scalar=N - 2 * COUNT_AIM,
                                                   in1=slope[:, :], op0=ALU.subtract, op1=ALU.mult)
                narrow(chained)
                if k == SEARCH_STEPS - 1:
                    return
                if k == 0:
                    chained(nc.vector.tensor_tensor(probe[:, 0, :], step_b[:, :], probe[:, 0, :], ALU.add))
                else:
                    between(chained)
                dve.sem_inc(probe_ready, 1)

            def narrow(chained):
                nc.vector.tensor_scalar(is_low[:, :], probe[:, 1, :], float(N - 2 * KTH), None, ALU.is_le)
                chained(nc.vector.tensor_scalar(is_high[:, :], probe[:, 1, :], float(N - 2 * KTH), None, ALU.is_gt))
                for side, m in ((0, is_low), (1, is_high)):
                    last = nc.vector.copy_predicated(bracket[:, side, :, :],
                                                     m[:, :].unsqueeze(1).to_broadcast([P, 2, NT]), probe[:, :, :])
                chained(last)

            def between(chained):
                low, high = bracket[:, 0], bracket[:, 1]
                nc.vector.tensor_tensor(step_c[:, :], high[:, 0, :], low[:, 0, :], ALU.subtract)
                chained(nc.vector.tensor_tensor(step_a[:, :], low[:, 1, :], high[:, 1, :], ALU.subtract))
                chained(nc.vector.reciprocal(step_b[:, :], step_a[:, :]))
                chained(nc.vector.scalar_tensor_tensor(out=step_b[:, :], in0=low[:, 1, :], scalar=N - 2 * COUNT_AIM,
                                                       in1=step_b[:, :], op0=ALU.subtract, op1=ALU.mult))
                chained(nc.vector.scalar_tensor_tensor(out=step_b[:, :], in0=step_b[:, :], scalar=1.0,
                                                       in1=step_c[:, :], op0=ALU.min, op1=ALU.mult))
                chained(nc.vector.tensor_tensor(probe[:, 0, :], step_b[:, :], low[:, 0, :], ALU.add))

            def pick_again(b):
                def waited(ins):
                    dve.drain()

                rows, high_t = sim[b % 2], bracket[:, 1, 0, :]
                between(waited)
                for j in range(NT):
                    nc.vector.tensor_scalar(above[:, j, :], rows[:, j, :], probe[:, 0, j:j + 1], None,
                                            ALU.is_ge, ALU.add, accum_out=probe[:, 1, j:j + 1])
                dve.drain()
                waited(nc.vector.tensor_scalar(probe[:, 1, :], probe[:, 1, :], -2.0, float(N), ALU.mult, ALU.add))
                narrow(waited)
                waited(nc.vector.tensor_scalar(need[:, :], bracket[:, 1, 1, :], 0.5, float(KTH - 1 - N // 2),
                                               ALU.mult, ALU.add))
                for j in range(NT):
                    waited(nc.vector.tensor_scalar(above[:, j, :], rows[:, j, :], high_t[:, j:j + 1], None, ALU.is_gt))
                    waited(nc.vector.scalar_tensor_tensor(out=below[0][:, :], in0=above[:, j, :], scalar=-BIG,
                                                          in1=rows[:, j, :], op0=ALU.mult, op1=ALU.add))
                    waited(nc.vector.max(top8[:, j, :], below[0][:, :]))
                waited(nc.vector.tensor_tensor(pick8[:, :, :], iota_row[:, 0:8].unsqueeze(1).to_broadcast([P, NT, 8]),
                                               need[:, :].unsqueeze(2).to_broadcast([P, NT, 8]), ALU.is_equal))
                waited(nc.vector.tensor_reduce(step_a[:, :], pick8[:, :, :], AX_X, ALU.add))
                waited(nc.vector.tensor_tensor(value8[:, :, :], pick8[:, :, :], top8[:, :, :], ALU.mult))
                waited(nc.vector.tensor_reduce(thr[:, :], value8[:, :, :], AX_X, ALU.add))
                waited(nc.vector.tensor_tensor(step_b[:, :], top8[:, :, 0], high_t, ALU.is_equal))
                waited(nc.vector.tensor_tensor(open_rows[:, :], step_a[:, :], step_b[:, :], ALU.is_le))
                waited(nc.vector.tensor_reduce(step_a[:, 0:1], open_rows[:, :], AX_X, ALU.add))
                for q in range(4):
                    waited(nc.vector.tensor_copy(open_q[:, q:q + 1], step_a[32 * q:32 * q + 32, 0:1]))
                waited(nc.vector.transpose(open_t[:, :], open_q[:, :]))
                waited(nc.vector.tensor_reduce(open_q[:, 0:1], open_t[:, :], AX_X, ALU.max))
                waited(nc.vector.transpose(open_t[:, :], open_q[:, :]))
                waited(nc.vector.tensor_reduce(open_q[0:1, 0:1], open_t[0:1, 0:4], AX_X, ALU.max))
                waited(nc.vector.tensor_copy(open_i[:, :], open_q[0:1, 0:1]))
                return dve.value_load(open_i[0:1, 0:1], min_val=0, max_val=NT)

            def take_away(b):
                rows = sim[b % 2]
                rest = below[0]
                for j in range(NT):
                    nc.vector.tensor_copy(rest[:, :], rows[:, j, :])
                    dve.drain()
                    with dve.Fori(0, (KTH - 1) // 8):
                        nc.vector.max(top8[:, j, :], rest[:, :])
                        dve.drain()
                        nc.vector.match_replace(rest[:, :], top8[:, j, :], rest[:, :], -BIG)
                        dve.drain()
                    nc.vector.max(top8[:, j, :], rest[:, :])
                    dve.drain()
                    nc.vector.tensor_copy(thr[:, j:j + 1], top8[:, j, (KTH - 1) % 8:(KTH - 1) % 8 + 1])
                    dve.drain()

            def threshold(b):
                rows = sim[b % 2]
                high_t = bracket[:, 1, 0, :]
                for j in range(NT):
                    last = nc.vector.tensor_scalar(above[:, j, :], rows[:, j, :], high_t[:, j:j + 1], None, ALU.is_gt)
                needed = mark(nc.vector.tensor_scalar(need[:, :], bracket[:, 1, 1, :], 0.5, float(KTH - 1 - N // 2),
                                                      ALU.mult, ALU.add))
                after(needed)

                def lowered(j):
                    return mark(nc.vector.scalar_tensor_tensor(out=below[j % 2][:, :], in0=above[:, j, :], scalar=-BIG,
                                                               in1=rows[:, j, :], op0=ALU.mult, op1=ALU.add))

                def eight(j):
                    return mark(nc.vector.max(top8[:, j, :], below[j % 2][:, :]))

                first = [lowered(0), lowered(1)]
                after(first[0])
                first[0] = eight(0)
                after(first[1])
                first[1] = eight(1)
                after(first[0])
                second = [lowered(2)]
                after(first[1])
                second.append(lowered(3))
                after(second[0])
                second[0] = eight(2)
                picking = mark(nc.vector.tensor_tensor(pick8[:, :, :],
                                                       iota_row[:, 0:8].unsqueeze(1).to_broadcast([P, NT, 8]),
                                                       need[:, :].unsqueeze(2).to_broadcast([P, NT, 8]), ALU.is_equal))
                after(second[1])
                second[1] = eight(3)
                after(picking)
                found = mark(nc.vector.tensor_reduce(step_a[:, :], pick8[:, :, :], AX_X, ALU.add))
                after(second[1])
                picking = mark(nc.vector.tensor_tensor(value8[:, :, :], pick8[:, :, :], top8[:, :, :], ALU.mult))
                opened = mark(nc.vector.tensor_tensor(step_b[:, :], top8[:, :, 0], high_t, ALU.is_equal))
                after(opened)
                after(found)
                opened = mark(nc.vector.tensor_tensor(open_rows[:, :], step_a[:, :], step_b[:, :], ALU.is_le))
                after(picking)
                picking = mark(nc.vector.tensor_reduce(thr[:, :], value8[:, :, :], AX_X, ALU.add))
                after(opened)
                opened = mark(nc.vector.tensor_reduce(step_a[:, 0:1], open_rows[:, :], AX_X, ALU.add))
                after(opened)
                for q in range(4):
                    opened = mark(nc.vector.tensor_copy(open_q[:, q:q + 1], step_a[32 * q:32 * q + 32, 0:1]))
                after(opened)
                opened = mark(nc.vector.transpose(open_t[:, :], open_q[:, :]))
                after(opened)
                opened = mark(nc.vector.tensor_reduce(open_q[:, 0:1], open_t[:, :], AX_X, ALU.max))
                after(opened)
                opened = mark(nc.vector.transpose(open_t[:, :], open_q[:, :]))
                after(opened)
                opened = mark(nc.vector.tensor_reduce(open_q[0:1, 0:1], open_t[0:1, 0:4], AX_X, ALU.max))
                after(opened)
                chained(nc.vector.tensor_copy(open_i[:, :], open_q[0:1, 0:1]))
                rows_open = dve.value_load(open_i[0:1, 0:1], min_val=0, max_val=NT)
                with dve.If(rows_open > 0):
                    still_open = pick_again(b)
                    with dve.If(still_open > 0):
                        take_away(b)

            def adjacency(b):
                dve.wait_ge(sig_ready, b + 1)
                for j in range(NT):
                    nc.vector.scalar_tensor_tensor(out=adj[:, j, :], in0=sim[b % 2][:, j, :], scalar=thr[:, j:j + 1],
                                                   in1=adj[:, j, :], op0=ALU.is_ge, op1=ALU.mult).then_inc(adj_ready, 1)

            def residual(b):
                def behind(j):
                    which, k = turns[("adjT", b, j)]
                    dve.wait_ge(drained[which], k + 1)
                    return nc.vector.bn_stats(bn[:, j, :], x_sb[b][:, j, :])

                for j in range(NT):
                    dve.wait_ge(adj_added, NT * b + j + 1)
                    src, free = given(("adjT", b, j))
                    nc.vector.tensor_tensor(x_sb[b][:, j, :], x_sb[b][:, j, :], src[:, :], ALU.add).then_inc(free, 1)
                    if j:
                        behind(j - 1)
                aggregate(behind(NT - 1), mv_y, x1_stats)

            def choose(b):
                dve.wait_ge(rough_ready, b + 1)
                chained(nc.vector.reciprocal(soft[:, :, :], rough[:, :, :]))
                chained(nc.vector.tensor_tensor(soft[:, :, :], soft[:, :, :], score[:, :, :], ALU.mult))
                chained(nc.vector.tensor_tensor(score[:, :, :], soft[:, :, :], rough[:, :, :], ALU.add))
                chained(nc.vector.scalar_tensor_tensor(out=biased[:, :, :], in0=score[:, :, :], scalar=0.5,
                                                       in1=bias_b[:, :].unsqueeze(1).to_broadcast([P, NT, E]),
                                                       op0=ALU.mult, op1=ALU.add))
                for j in range(NT):
                    last = nc.vector.max(best[:, j, :], biased[:, j, :])
                chained(last)
                for j in range(NT):
                    last = nc.vector.max_index(best_i[:, j, :], best[:, j, :], biased[:, j, :])
                chained(last)
                chained(nc.vector.tensor_copy(choice[:, :, :], best_i[:, :, 0:2].rearrange("p j k -> p k j")))
                for k in range(2):
                    last = nc.vector.tensor_tensor(onehot[:, k, :, :],
                                                   iota_row[:, 0:E].unsqueeze(1).to_broadcast([P, NT, E]),
                                                   choice[:, k, :].unsqueeze(2).to_broadcast([P, NT, E]), ALU.is_equal)
                chained(last)
                for k in range(2):
                    nc.vector.tensor_tensor(picked[:, k, :, :], onehot[:, k, :, :], score[:, :, :], ALU.mult)
                chained(nc.vector.tensor_tensor(mask[:, :, :], onehot[:, 0, :, :], onehot[:, 1, :, :], ALU.add))
                if b:
                    chained(nc.vector.tensor_copy(before[:, 0, :], before[:, NT, :]))
                for j in range(NT):
                    chained(nc.vector.tensor_tensor(before[:, j + 1, :], before[:, j, :], mask[:, j, :], ALU.add))
                dve.sem_inc(mask_ready, 1)
                mark(nc.vector.tensor_reduce(weight[:, :, :], picked[:, :, :, :], AX_X, ALU.add))

            def place_tokens(b):
                src, free = given(("place", b))
                chained(nc.vector.tensor_copy(place[:, :, :], src[:, 0:NT * E].rearrange("p (j e) -> p j e", j=NT)))
                dve.sem_inc(free, 1)
                nc.vector.tensor_tensor(total[:, :], weight[:, 0, :], weight[:, 1, :], ALU.add)
                for k in range(2):
                    last = nc.vector.tensor_tensor(picked[:, k, :, :], onehot[:, k, :, :], place[:, :, :], ALU.mult)
                chained(last)
                nc.vector.reciprocal(total[:, :], total[:, :])
                chained(nc.vector.tensor_reduce(slot[:, :, :], picked[:, :, :, :], AX_X, ALU.add))
                for k in range(2):
                    nc.vector.tensor_tensor(weight[:, k, :], weight[:, k, :], total[:, :], ALU.mult)
                chained(nc.vector.tensor_scalar(upper_half[:, :, :], slot[:, :, :], float(P), None, ALU.is_ge))
                chained(nc.vector.scalar_tensor_tensor(out=slot[:, :, :], in0=upper_half[:, :, :], scalar=-float(P),
                                                       in1=slot[:, :, :], op0=ALU.mult, op1=ALU.add))
                chained(nc.vector.scalar_tensor_tensor(out=column[:, :, :], in0=choice[:, :, :], scalar=float(HALVES),
                                                       in1=upper_half[:, :, :], op0=ALU.mult, op1=ALU.add))
                nc.vector.tensor_tensor(row_hot[:, :, :, :],
                                        iota_row[:, :].unsqueeze(1).unsqueeze(1).to_broadcast([P, 2, NT, P]),
                                        slot[:, :, :].unsqueeze(3).to_broadcast([P, 2, NT, P]), ALU.is_equal)
                each = [P, 2, NT, COLS]
                last = nc.vector.tensor_tensor(col_hot[:, 2], iota_row[:, 0:COLS].unsqueeze(1).unsqueeze(1).to_broadcast(each),
                                               column[:, :, :].unsqueeze(3).to_broadcast(each), ALU.is_equal)
                chained(last)
                tokens = token_id[:, NT * b:NT * b + NT]
                nc.vector.tensor_tensor(col_hot[:, 0], col_hot[:, 2],
                                        tokens.unsqueeze(1).unsqueeze(3).to_broadcast(each), ALU.mult)
                last = nc.vector.tensor_tensor(col_hot[:, 1], col_hot[:, 2],
                                               weight[:, :, :].unsqueeze(3).to_broadcast(each), ALU.mult)
                chained(last)
                dve.sem_inc(hot_ready, 1)
                if b == 0:
                    for a in range(HALVES):
                        chained(nc.vector.tensor_scalar(spare[:, a, :], place[:, a, :], token_id[:, a:a + 1],
                                                        float(CAP - 1), ALU.subtract, ALU.add))
                        chained(nc.vector.scalar_tensor_tensor(out=spare[:, a, :], in0=mask[:, a, :],
                                                               scalar=float(2 * CAP), in1=spare[:, a, :],
                                                               op0=ALU.mult, op1=ALU.add))

            def spare_slots(a):
                for e in range(E):
                    last = nc.vector.tensor_scalar(spare_hot[a][:, e, :], iota_slot[:, :], spare[:, a, e:e + 1],
                                                   None, ALU.is_equal)
                last.then_inc(spare_hot_ready, 1)

            def add_spare():
                src, free = given(("spare",))
                chained(nc.vector.tensor_copy(spare_tab[:, :], src[:, 0:COLS]))
                chained(nc.vector.tensor_tensor(spare_tab[:, :], spare_tab[:, :], src[:, COLS:2 * COLS], ALU.add))
                dve.sem_inc(free, 1)

            def add_table(b):
                src, free = given(("table", b))
                got = src[:, 0:3 * COLS].rearrange("p (v c) -> p v c", v=3)
                if b == 0:
                    chained(nc.vector.tensor_copy(table[:, :, :], got))
                else:
                    chained(nc.vector.tensor_tensor(table[:, :, :], table[:, :, :], got, ALU.add))
                dve.sem_inc(free, 1)

            def rows_low(which, count, dst, free):
                dve.wait_ge(xT_hi_ready, count)
                hi, lo = dst
                nc.vector.tensor_tensor(lo, which[:, :].rearrange("p (c t) -> p c t", c=DK), hi.bitcast(F32),
                                        ALU.subtract).then_inc(free, 1)

            def batch_rows_low(b, tiles):
                for j in tiles:
                    src, free = given(("xT", b, j))
                    at = slice((j % 2) * P, (j % 2 + 1) * P)
                    rows_low(src, NT * b + j + 1, (xT_hi[j // 2][:, :, at], xT_lo[j // 2][:, :, at]), free)

            def weight_low(k, s, count):
                raw, hi, lo = weight_parts(s)[k]
                dve.wait_ge(w_hi_ready, count)
                nc.vector.tensor_tensor(lo[:, :, :], raw[:, :, :], hi[:, :, :].bitcast(F32),
                                        ALU.subtract).then_inc(w_split, 1)

            nc.vector.memset(before[:, 0, :], 0.0)
            nc.vector.memset(open_q[:, :], 0.0)
            prepare(0)
            start(0)
            for k in range(SEARCH_STEPS):
                search(0, k)
            for b in range(B):
                more = b + 1 < B
                threshold(b)
                adjacency(b)
                residual(b)
                if b:
                    choose(b - 1)
                if more:
                    prepare(b + 1)
                if more:
                    start(b + 1)
                    search(b + 1, 0)
                if b:
                    if more:
                        search(b + 1, 1)
                    place_tokens(b - 1)
                batch_rows_low(b, (0, 1))
                if more:
                    search(b + 1, 2 if b else 1)
                if b:
                    add_table(b - 1)
                batch_rows_low(b, (2, 3))
                if more:
                    if b == 0:
                        search(b + 1, 2)
                    search(b + 1, 3)
            for a in range(HALVES):
                spare_slots(a)
            add_spare()
            choose(B - 1)
            place_tokens(B - 1)
            weight_low(0, 0, 1)
            weight_low(1, 0, 2)
            add_table(B - 1)
            chained(nc.vector.tensor_scalar(table[:, 2, :], table[:, 2, :], -1.0, 1.0, ALU.mult, ALU.add))
            chained(nc.vector.tensor_tensor(spare_tab[:, :], spare_tab[:, :], table[:, 2, :], ALU.mult))
            nc.vector.tensor_tensor(slot_token[:, :], spare_tab[:, :], table[:, 0, :], ALU.add).then_inc(table_ready, 1)
            weight_low(2, 0, 3)

            def slot_rows_low(n, r):
                for a in range(HALVES):
                    at = slice(a * P, (a + 1) * P)
                    rows_low(bank[f"t{a}"], HALVES * n + a + 1, (xT_hi[r][:, :, at], xT_lo[r][:, :, at]),
                             drained[f"t{a}"])

            def product(n, m):
                rows = rows_of(m)
                dve.wait_ge(silu_ready, MI * n + m + 1)
                nc.vector.tensor_tensor(hidden[0:rows, m, :], silu_g[0:rows, m, :], gu_bank[m][0:rows, CAP:2 * CAP],
                                        ALU.mult).then_inc(h_ready, 1)

            def hidden_low(n, m):
                rows = rows_of(m)
                dve.wait_ge(h_hi_ready, MI * n + m + 1)
                nc.vector.tensor_tensor(hidden_lo[0:rows, m, :], hidden[0:rows, m, :],
                                        hidden_hi[0:rows, m, :].bitcast(F32), ALU.subtract).then_inc(h_split, 1)

            def expert(i, r, more):
                n = SHARED + 2 * i + r
                e = 2 * i + r
                if more:
                    weight_low(0, 1 - r, 3 * e + 4)
                product(n, 0)
                hidden_low(n, 0)
                if more:
                    weight_low(1, 1 - r, 3 * e + 5)
                product(n, 1)
                hidden_low(n, 1)
                if more:
                    weight_low(2, 1 - r, 3 * e + 6)
                product(n, 2)
                hidden_low(n, 2)
                if more:
                    slot_rows_low(n + 1, 1 - r)

            slot_rows_low(SHARED, 0)
            with dve.Fori(0, E // 2 - 1) as i:
                expert(i, 0, True)
                expert(i, 1, True)
            expert(E // 2 - 1, 0, True)
            expert(E // 2 - 1, 1, False)

        @block.gpsimd
        def _(pool):
            steps = Count()

            def chained(ins):
                ins.then_inc(pool_step, 1)
                pool.wait_ge(pool_step, steps.up())

            chained(nc.gpsimd.memset(ones[:, :], 1.0))
            chained(nc.gpsimd.affine_select(out=ident[:, :], in_=ones[:, :], compare_op=ALU.is_equal, fill=0.0,
                                            base=0, pattern=[[1, P]], channel_multiplier=-1))
            chained(nc.gpsimd.affine_select(out=upper[:, :], in_=ones[:, :], compare_op=ALU.is_gt, fill=0.0,
                                            base=0, pattern=[[1, P]], channel_multiplier=-1))
            nc.gpsimd.memset(half_power[:, :], 0.5)
            nc.gpsimd.memset(neg_half_power[:, :], -0.5)
            nc.gpsimd.iota(iota_row[:, :], pattern=[[1, P]], base=0, channel_multiplier=0,
                           allow_small_or_imprecise_dtypes=True)
            nc.gpsimd.iota(iota_slot[:, :], pattern=[[1, CAP]], base=0, channel_multiplier=0,
                           allow_small_or_imprecise_dtypes=True)
            nc.gpsimd.iota(token_id16[:, :], pattern=[[P, HALVES]], base=0, channel_multiplier=1,
                           allow_small_or_imprecise_dtypes=True)
            chained(nc.gpsimd.iota(token_id[:, :], pattern=[[P, TILES]], base=0, channel_multiplier=1,
                                   allow_small_or_imprecise_dtypes=True))
            pool.sem_inc(consts_ready, 1)
            chained(nc.gpsimd.memset(w2_raw[LAST:P, MI - 1, :], 0.0))
            pool.sem_inc(pads_ready, 1)

            def shared_low(some):
                for k in some:
                    raw, hi, lo = weight_parts(1)[k]
                    pool.wait_ge(shared_hi_ready, k + 1)
                    nc.gpsimd.tensor_tensor(lo[:, :, :], raw[:, :, :], hi[:, :, :].bitcast(F32),
                                            ALU.subtract).then_inc(shared_split, 1)

            def spread(b):
                pool.wait_ge(sim_stats, b + 1)
                nc.gpsimd.tensor_tensor(std_s[:, :], mv_s[:, :, 1], half_power[:, 0:NT], ALU.pow).then_inc(std_ready, 1)

            def sigmoids(b):
                if b == 0:
                    pool.wait_ge(gamma_ready, 1)
                pool.wait_ge(tanh_ready, b + 1)
                nc.gpsimd.tensor_scalar(adj[:, :, :], adj[:, :, :], 1.0, gamma_c[:, 3:4],
                                        ALU.add, ALU.mult).then_inc(sig_ready, 1)

            def rstd(var):
                chained(nc.gpsimd.tensor_scalar(ln_a[:, :], var, EPS, 1.0, ALU.add, ALU.mult))
                chained(nc.gpsimd.tensor_tensor(ln_a[:, :], ln_a[:, :], neg_half_power[:, :], ALU.pow))

            def base(b):
                pool.wait_ge(x_stats, b + 1)
                chained(nc.gpsimd.tensor_scalar(x_var[:, :], x_moment[:, b % 2, 1, :], 1.0 / D, 0.0, ALU.mult, ALU.add))
                rstd(x_var[:, :])
                chained(nc.gpsimd.tensor_scalar(ln_a[:, :], ln_a[:, :], gamma_c[:, 2:3], 1.0, ALU.mult, ALU.mult))
                nc.gpsimd.tensor_tensor(ln_add[:, :], x_moment[:, b % 2, 0, :], ln_a[:, :], ALU.mult)
                chained(nc.gpsimd.tensor_scalar(ln_mul[:, :], ln_a[:, :], 1.0, 1.0, ALU.mult, ALU.add))
                for j in range(NT):
                    last = nc.gpsimd.tensor_scalar(x_sb[b][:, j, :], x_sb[b][:, j, :], ln_mul[:, j:j + 1],
                                                   ln_add[:, j:j + 1], ALU.mult, ALU.add)
                chained(last)

            def add_adjacency(b):
                for j in range(NT):
                    pool.wait_ge(adj_ready, NT * b + j + 1)
                    nc.gpsimd.tensor_tensor(x_sb[b][:, j, :], x_sb[b][:, j, :], adj[:, j, :],
                                            ALU.add).then_inc(adj_added, 1)

            def normed(b):
                pool.wait_ge(x1_stats, b + 1)
                if b:
                    pool.wait_ge(xn_stored, 16 * b)
                rstd(mv_y[:, :, 1])
                chained(nc.gpsimd.tensor_tensor(ln_add[:, :], mv_y[:, :, 0], ln_a[:, :], ALU.mult))
                chained(nc.gpsimd.tensor_scalar(ln_add[:, :], ln_add[:, :], -1.0, 0.0, ALU.mult, ALU.add))
                for j in range(NT):
                    nc.gpsimd.tensor_scalar(xn[:, j, :], x_sb[b][:, j, :], ln_a[:, j:j + 1],
                                            ln_add[:, j:j + 1], ALU.mult, ALU.add).then_inc(xn_ready, 1)
                pool.wait_ge(xn_ready, NT * (b + 1))

            def scores(b):
                pool.wait_ge(soft_ready, b + 1)
                if b:
                    pool.wait_ge(mask_ready, b)
                chained(nc.gpsimd.tensor_scalar(score[:, :, :], logit[:, :, :], 0.0, 1e-30, ALU.max, ALU.add))
                chained(nc.gpsimd.tensor_tensor(score[:, :, :], score[:, :, :], soft[:, :, :], ALU.add))
                pool.sem_inc(score_ready, 1)

            def hidden_values(n, next_b=None):
                def low(m):
                    rows = rows_of(m)
                    pool.wait_ge(h_hi_ready, MI * n + m + 1)
                    nc.gpsimd.tensor_tensor(hidden_lo[0:rows, m, :], hidden[0:rows, m, :],
                                            hidden_hi[0:rows, m, :].bitcast(F32), ALU.subtract).then_inc(h_split, 1)

                for m in range(MI):
                    rows = rows_of(m)
                    pool.wait_ge(u_ready, MI * n + m + 1)
                    pool.wait_ge(silu_ready, MI * n + m + 1)
                    nc.gpsimd.tensor_tensor(hidden[0:rows, m, :], silu_g[0:rows, m, :], up_u[0:rows, m, :],
                                            ALU.mult).then_inc(h_ready, 1)
                    if m:
                        low(m - 1)
                    if m == MI - 1 and next_b is not None:
                        sigmoids(next_b)
                low(MI - 1)

            def add_residual(n):
                b, half = n // 2, n % 2
                for a in range(HALVES):
                    pool.wait_ge(y_copied, HALVES * n + a + 1)
                    nc.gpsimd.tensor_tensor(y_sb[half][:, a, :], y_sb[half][:, a, :],
                                            x_sb[b][:, HALVES * half + a, :], ALU.add).then_inc(y_added, 1)

            def gather(e):
                r = e % 2
                for a in range(HALVES):
                    if e >= 2:
                        pool.wait_ge(filled[f"t{a}"], fills[f"t{a}"] + e - 1)
                    at = HALVES * e + a
                    nc.gpsimd.indirect_dma_start(
                        out=x_slots[r][:, a, :], out_offset=None, in_=xn_rows[:, :],
                        in_offset=bass.IndirectOffsetOnAxis(ap=slot_token[:, at:at + 1], axis=0),
                    ).then_inc(gathered[r][a], 16)

            def scatter(e):
                for a in range(HALVES):
                    at = HALVES * e + a
                    pool.wait_ge(y_copied, HALVES * (SHARED + e) + a + 1)
                    if at:
                        pool.wait_ge(scattered, 16 * at)
                    nc.gpsimd.indirect_dma_start(
                        out=out_rows[:, :], out_offset=bass.IndirectOffsetOnAxis(ap=slot_token[:, at:at + 1], axis=0),
                        in_=y_sb[e % 2][:, a, :], in_offset=None, compute_op=ALU.add,
                    ).then_inc(scattered, 16)

            pool.wait_ge(gate_hi_ready, 1)
            nc.gpsimd.tensor_tensor(gate_lo[:, :, :], gate_sb[:, :, :], gate_hi[:, :, :].bitcast(F32),
                                    ALU.subtract).then_inc(gate_split, 1)
            spread(0)
            sigmoids(0)
            base(0)
            add_adjacency(0)
            shared_low((0,))
            spread(1)
            shared_low((1,))
            normed(0)
            shared_low((2,))
            base(1)
            for b in range(B):
                more = b + 1 < B
                if not more:
                    scores(b)
                hidden_values(2 * b, b + 1 if more else None)
                if more:
                    scores(b)
                if more:
                    add_adjacency(b + 1)
                add_residual(2 * b)
                if b + 2 < B:
                    spread(b + 2)
                hidden_values(2 * b + 1)
                if more:
                    normed(b + 1)
                else:
                    pool.wait_ge(table_ready, 1)
                    pool.wait_ge(xn_stored, 16 * B)
                    gather(0)
                    gather(1)
                add_residual(2 * b + 1)
                if b + 2 < B:
                    base(b + 2)

            for r in range(2):
                pool.wait_ge(stored[r], 16 * (SHARED // 2))
            for e in range(E):
                if e + 2 < E:
                    gather(e + 2)
                scatter(e)


_OUT = (4, 512, 512)


def kernel(x, ctx_512, L0_xattn_Wq, L0_xattn_Wk, L0_xattn_gamma_raw, L0_ffn_input_ids, L0_ffn_gate_w, L0_ffn_gate_b,
           L0_ffn_W1, L0_ffn_W3, L0_ffn_W2, L0_ffn_Ws1, L0_ffn_Ws3, L0_ffn_Ws2):
    import concourse.bacc as _bacc
    from concourse.bass_utils import run_bass_kernel_spmd as _run

    def by_rows(w):
        w = np.swapaxes(np.asarray(w), -1, -2)
        w = w.reshape(w.shape[:-2] + (w.shape[-2] // P, P, w.shape[-1]))
        return np.swapaxes(w, -3, -2)

    laid = {
        "x": np.asarray(x),
        "ctxT": np.swapaxes(np.asarray(ctx_512), 1, 2),
        "WqT": np.asarray(L0_xattn_Wq).T,
        "WkT": np.asarray(L0_xattn_Wk).T,
        "gamma_raw": np.asarray(L0_xattn_gamma_raw).reshape(1),
        "gateT": np.asarray(L0_ffn_gate_w).T,
        "gate_b": np.asarray(L0_ffn_gate_b),
        "W1T": by_rows(L0_ffn_W1),
        "W3T": by_rows(L0_ffn_W3),
        "W2T": np.swapaxes(np.asarray(L0_ffn_W2), 1, 2),
        "Ws1T": by_rows(L0_ffn_Ws1),
        "Ws3T": by_rows(L0_ffn_Ws3),
        "Ws2T": np.asarray(L0_ffn_Ws2).T,
    }
    nc = _bacc.Bacc("TRN2", target_bir_lowering=False, num_devices=1)
    arrays, args = {}, []
    for name, a in laid.items():
        a = np.ascontiguousarray(a)
        arrays[f"in_{name}"] = a
        args.append(nc.dram_tensor(f"in_{name}", a.shape, mybir.dt.from_np(a.dtype), kind="ExternalInput").ap())
    args.append(nc.dram_tensor("out_0", _OUT, F32, kind="ExternalOutput").ap())
    build(nc, *args)
    r = _run(nc, [arrays], core_ids=[0])
    return r.results[0]["out_0"]
```
